# Optimizing a Trainium2 kernel written in Bass

```python
import numpy as np
import jax
import jax.numpy as jnp

def _softmax(x, axis=-1):
    return jax.nn.softmax(x, axis=axis)

def _gelu(x):
    return jax.nn.gelu(x, approximate=True)

def _silu(x):
    return jax.nn.silu(x)

def _sigmoid(x):
    return jax.nn.sigmoid(x)

def _layernorm(x, axis=-1, eps=1e-05):
    m = jnp.mean(x, axis=axis, keepdims=True)
    v = jnp.var(x, axis=axis, keepdims=True)
    return (x - m) / jnp.sqrt(v + eps)

def _scatter_add(tgt, idx, src, axis=0):
    return tgt.at[idx].add(src)

def _segment_sum(src, seg, n):
    return jax.ops.segment_sum(src, seg, n)
kernel_name = 'mk_xattn_ffn_d2_seqx_r8_9a1ffc'

def setup_inputs(seed: int=0):
    np.random.seed(seed)
    _w = jnp.asarray

    def _rec_inputs():
        import jax
        import jax.numpy as jnp
        _rk = jax.random.key(seed)
        x = -0.0002928 + 1 * jax.random.normal(jax.random.fold_in(_rk, 1), (32, 128, 128), jnp.float32)
        _lenS = 128 - jax.random.randint(jax.random.fold_in(_rk, 7), (32,), 0, max(1, 128 // 4) + 1, jnp.int32)
        _lenS2 = 128 - jax.random.randint(jax.random.fold_in(_rk, 8), (32,), 0, max(1, 128 // 4) + 1, jnp.int32)
        _ctx_1024P = jax.random.normal(jax.random.fold_in(_rk, 11), (32, 16, 128), jnp.float32)
        _ctx_1024c = jax.random.dirichlet(jax.random.fold_in(_rk, 511), 0.3 * jnp.ones((16,), jnp.float32), (32, 128))
        _ctx_1024t = jnp.einsum('bsk,bkd->bsd', _ctx_1024c, _ctx_1024P)
        _ctx_1024t = _ctx_1024t * jax.lax.rsqrt(jnp.mean(jnp.square(_ctx_1024t)) + 1e-12) * 0.953939
        ctx_1024 = -1.39393e-06 + 0.999914 * (_ctx_1024t + 0.3 * jax.random.normal(jax.random.fold_in(_rk, 611), (32, 128, 128), jnp.float32))
        _validS = jnp.arange(128)[None, :] < _lenS[:, None]
        _validS2 = jnp.arange(128)[None, :] < _lenS2[:, None]
        _causal = jnp.tril(jnp.ones((128, 128), dtype=bool))
        mask_BxS2_if1 = jnp.where(jnp.ones((32, 128), dtype=bool), 1, 0).astype(jnp.int32)
        mask_Bx1xSxS2_ff0 = jnp.where(jnp.ones((32, 1, 128, 128), dtype=bool), 0.0, -1000000000.0).astype(jnp.float32)
        return (x, ctx_1024, mask_BxS2_if1, mask_Bx1xSxS2_ff0)
    x, ctx_1024, mask_BxS2_if1, mask_Bx1xSxS2_ff0 = _rec_inputs()

    def _L0_xattn_setup():
        import jax, jax.numpy as jnp
        import numpy as np
        D_MODEL = 128
        N_HEADS = 16
        D_K = D_MODEL // N_HEADS
        B, L = (2, 256)

        def _dense_bf16(x, W, b):
            return jnp.matmul(x.astype(jnp.bfloat16), W.astype(jnp.bfloat16)) + b.astype(jnp.bfloat16)

        def _attention(q, k, v, mask):
            Lq, Ls, dk = (q.shape[2], k.shape[2], q.shape[3])
            scale = 1.0 / np.sqrt(dk)
            scores = jnp.einsum('bhqd,bhkd->bhqk', q, k) * scale
            causal = jnp.tril(jnp.ones((Lq, Ls), bool))
            full_mask = causal[None, None] & (mask[:, None, None, :] > 0)
            scores = jnp.where(full_mask, scores, -jnp.inf)
            p = jax.nn.softmax(scores, axis=-1)
            return jnp.einsum('bhqk,bhkd->bhqd', p, v)
        key = jax.random.key(seed)
        ks = jax.random.split(key, 8)
        inp = {'q': jax.random.normal(ks[0], (B, L, D_MODEL), jnp.float32), 'k': jax.random.normal(ks[1], (B, L, D_MODEL), jnp.float32), 'v': jax.random.normal(ks[2], (B, L, D_MODEL), jnp.float32), 'mask': jnp.ones((B, L), jnp.int32), 'Wq': jax.random.normal(ks[3], (D_MODEL, D_MODEL), jnp.float32) * 0.02, 'bq': jnp.zeros((D_MODEL,), jnp.float32), 'Wk': jax.random.normal(ks[4], (D_MODEL, D_MODEL), jnp.float32) * 0.02, 'bk': jnp.zeros((D_MODEL,), jnp.float32), 'Wv': jax.random.normal(ks[5], (D_MODEL, D_MODEL), jnp.float32) * 0.02, 'bv': jnp.zeros((D_MODEL,), jnp.float32), 'Wo': jax.random.normal(ks[6], (D_MODEL, D_MODEL), jnp.float32) * 0.02, 'bo': jnp.zeros((D_MODEL,), jnp.float32)}
        return inp
    _L0_xattn_all = _L0_xattn_setup()
    _L0_xattn_in = {k: v for k, v in _L0_xattn_all.items() if k in ('Wq', 'bq', 'Wk', 'bk', 'Wv', 'bv', 'Wo', 'bo')}
    del _L0_xattn_all

    def _L0_ffn_setup():
        import jax, jax.numpy as jnp
        import numpy as np
        D_MODEL = 128
        EXPERT_DIM = 64
        N_EXPERTS = 8
        TOP_K = 2

        def _sq_relu(h):
            return jnp.square(jax.nn.relu(h))
        key = jax.random.key(seed)
        ks = jax.random.split(key, 6)
        s = 0.02
        x = jax.random.normal(ks[0], (2, 256, D_MODEL), dtype=jnp.float32)
        Ws1 = jax.random.normal(ks[1], (D_MODEL, EXPERT_DIM), dtype=jnp.float32) * s
        Ws2 = jax.random.normal(ks[2], (EXPERT_DIM, D_MODEL), dtype=jnp.float32) * s
        W1 = jax.random.normal(ks[3], (N_EXPERTS, D_MODEL, EXPERT_DIM), dtype=jnp.float32) * s
        W2 = jax.random.normal(ks[4], (N_EXPERTS, EXPERT_DIM, D_MODEL), dtype=jnp.float32) * s
        Wr = jax.random.normal(ks[5], (D_MODEL, N_EXPERTS), dtype=jnp.float32) * s
        return {'x': x, 'Ws1': Ws1, 'Ws2': Ws2, 'W1': W1, 'W2': W2, 'Wr': Wr}
    _L0_ffn_all = _L0_ffn_setup()
    _L0_ffn_in = {k: v for k, v in _L0_ffn_all.items() if k in ('Ws1', 'Ws2', 'W1', 'W2', 'Wr')}
    del _L0_ffn_all

    def _L1_xattn_setup():
        import jax, jax.numpy as jnp
        import numpy as np
        HIDDEN = 128
        HEADS = 16
        HEAD_DIM = HIDDEN // HEADS
        B, F, T = (2, 256, 256)
        key = jax.random.key(seed)
        ks = jax.random.split(key, 6)
        return {'query_input': jax.random.normal(ks[0], (B, F, HIDDEN), dtype=jnp.float32), 'source_input': jax.random.normal(ks[1], (B, T, HIDDEN), dtype=jnp.float32), 'bias': jnp.zeros((B, 1, F, T), dtype=jnp.float32), 'wq': jax.random.normal(ks[2], (HIDDEN, HEADS, HEAD_DIM), dtype=jnp.float32) * HIDDEN ** (-0.5), 'wk': jax.random.normal(ks[3], (HIDDEN, HEADS, HEAD_DIM), dtype=jnp.float32) * HIDDEN ** (-0.5), 'wv': jax.random.normal(ks[4], (HIDDEN, HEADS, HEAD_DIM), dtype=jnp.float32) * HIDDEN ** (-0.5), 'wo': jax.random.normal(ks[5], (HEADS, HEAD_DIM, HIDDEN), dtype=jnp.float32) * HIDDEN ** (-0.5)}
    _L1_xattn_all = _L1_xattn_setup()
    _L1_xattn_in = {k: v for k, v in _L1_xattn_all.items() if k in ('wq', 'wk', 'wv', 'wo')}
    del _L1_xattn_all

    def _L1_ffn_setup():
        import jax, jax.numpy as jnp
        import numpy as np
        B, S, D = (2, 256, 128)
        H, E, P, K = (8, 8, 128, 2)
        SCALE = 1.0 / np.sqrt(P)

        def _get_sel_gate(x, w, route_scale):
            logits = jnp.einsum('bsd,ed->bse', x, w).astype(jnp.float32)
            raw = logits.reshape(x.shape[0], x.shape[1], H, E)
            probs = jax.nn.sigmoid(raw)
            vals, idx = jax.lax.top_k(probs, K)
            vals = vals / jnp.clip(vals.sum(-1, keepdims=True), 1e-09)
            vals = vals * route_scale
            gate = (jax.nn.one_hot(idx, E, dtype=vals.dtype) * vals[..., None]).sum(-2)
            return gate
        key = jax.random.key(seed)
        ks = jax.random.split(key, 8)
        std = 1.0 / np.sqrt(D)
        return {'x': jax.random.normal(ks[0], (B, S, D), jnp.float32), 'q_w': jax.random.normal(ks[1], (H * P, D), jnp.float32) * std, 'k_w': jax.random.normal(ks[2], (H * P, D), jnp.float32) * std, 'v_w': jax.random.normal(ks[3], (H * E, D, P), jnp.float32) * std, 'o_w': jax.random.normal(ks[4], (H * E, P, D), jnp.float32) * (1.0 / np.sqrt(H * P)), 'sel_v_w': jax.random.normal(ks[5], (H * E, D), jnp.float32) * std, 'sel_o_w': jax.random.normal(ks[6], (H * E, D), jnp.float32) * std, 'route_scale': jnp.ones((1,), jnp.float32)}
    _L1_ffn_all = _L1_ffn_setup()
    _L1_ffn_in = {k: v for k, v in _L1_ffn_all.items() if k in ('q_w', 'k_w', 'v_w', 'o_w', 'sel_v_w', 'sel_o_w', 'route_scale')}
    del _L1_ffn_all
    return {'x': x, 'ctx_1024': ctx_1024, 'mask_BxS2_if1': mask_BxS2_if1, 'mask_Bx1xSxS2_ff0': mask_Bx1xSxS2_ff0, 'L0_xattn_Wq': _L0_xattn_in['Wq'], 'L0_xattn_bq': _L0_xattn_in['bq'], 'L0_xattn_Wk': _L0_xattn_in['Wk'], 'L0_xattn_bk': _L0_xattn_in['bk'], 'L0_xattn_Wv': _L0_xattn_in['Wv'], 'L0_xattn_bv': _L0_xattn_in['bv'], 'L0_xattn_Wo': _L0_xattn_in['Wo'], 'L0_xattn_bo': _L0_xattn_in['bo'], 'L0_ffn_Ws1': _L0_ffn_in['Ws1'], 'L0_ffn_Ws2': _L0_ffn_in['Ws2'], 'L0_ffn_W1': _L0_ffn_in['W1'], 'L0_ffn_W2': _L0_ffn_in['W2'], 'L0_ffn_Wr': _L0_ffn_in['Wr'], 'L1_xattn_wq': _L1_xattn_in['wq'], 'L1_xattn_wk': _L1_xattn_in['wk'], 'L1_xattn_wv': _L1_xattn_in['wv'], 'L1_xattn_wo': _L1_xattn_in['wo'], 'L1_ffn_q_w': _L1_ffn_in['q_w'], 'L1_ffn_k_w': _L1_ffn_in['k_w'], 'L1_ffn_v_w': _L1_ffn_in['v_w'], 'L1_ffn_o_w': _L1_ffn_in['o_w'], 'L1_ffn_sel_v_w': _L1_ffn_in['sel_v_w'], 'L1_ffn_sel_o_w': _L1_ffn_in['sel_o_w'], 'L1_ffn_route_scale': _L1_ffn_in['route_scale']}

def reference(x, ctx_1024, mask_BxS2_if1, mask_Bx1xSxS2_ff0, L0_xattn_Wq, L0_xattn_bq, L0_xattn_Wk, L0_xattn_bk, L0_xattn_Wv, L0_xattn_bv, L0_xattn_Wo, L0_xattn_bo, L0_ffn_Ws1, L0_ffn_Ws2, L0_ffn_W1, L0_ffn_W2, L0_ffn_Wr, L1_xattn_wq, L1_xattn_wk, L1_xattn_wv, L1_xattn_wo, L1_ffn_q_w, L1_ffn_k_w, L1_ffn_v_w, L1_ffn_o_w, L1_ffn_sel_v_w, L1_ffn_sel_o_w, L1_ffn_route_scale):
    import jax
    import jax.numpy as jnp

    def _L0_xattn_ref(q, k, v, mask, Wq, bq, Wk, bk, Wv, bv, Wo, bo):
        import jax, jax.numpy as jnp
        import numpy as np
        D_MODEL = 128
        N_HEADS = 16
        D_K = D_MODEL // N_HEADS
        B, L = (2, 256)

        def _dense_bf16(x, W, b):
            return jnp.matmul(x.astype(jnp.bfloat16), W.astype(jnp.bfloat16)) + b.astype(jnp.bfloat16)

        def _attention(q, k, v, mask):
            Lq, Ls, dk = (q.shape[2], k.shape[2], q.shape[3])
            scale = 1.0 / np.sqrt(dk)
            scores = jnp.einsum('bhqd,bhkd->bhqk', q, k) * scale
            causal = jnp.tril(jnp.ones((Lq, Ls), bool))
            full_mask = causal[None, None] & (mask[:, None, None, :] > 0)
            scores = jnp.where(full_mask, scores, -jnp.inf)
            p = jax.nn.softmax(scores, axis=-1)
            return jnp.einsum('bhqk,bhkd->bhqd', p, v)
        query = _dense_bf16(q, Wq, bq).astype(jnp.float32)
        key_p = _dense_bf16(k, Wk, bk).astype(jnp.float32)
        val_p = _dense_bf16(v, Wv, bv).astype(jnp.float32)
        Bb, Lt, _ = query.shape
        Ls = key_p.shape[1]
        query = query.reshape(Bb, Lt, N_HEADS, D_K).transpose(0, 2, 1, 3)
        key_p = key_p.reshape(Bb, Ls, N_HEADS, D_K).transpose(0, 2, 1, 3)
        val_p = val_p.reshape(Bb, Ls, N_HEADS, D_K).transpose(0, 2, 1, 3)
        x = _attention(query, key_p, val_p, mask)
        x = x.transpose(0, 2, 1, 3).reshape(Bb, Lt, D_MODEL)
        out = _dense_bf16(x, Wo, bo)
        return out.astype(jnp.float32)

    def _L0_ffn_ref(x, Ws1, Ws2, W1, W2, Wr):
        import jax, jax.numpy as jnp
        import numpy as np
        D_MODEL = 128
        EXPERT_DIM = 64
        N_EXPERTS = 8
        TOP_K = 2

        def _sq_relu(h):
            return jnp.square(jax.nn.relu(h))
        shape = x.shape
        xf = x.reshape(-1, D_MODEL)
        out_shared = _sq_relu(xf @ Ws1) @ Ws2
        logits = xf @ Wr
        top_vals, top_idx = jax.lax.top_k(logits, TOP_K)
        rw = jax.nn.softmax(top_vals.astype(jnp.float32), axis=-1).astype(x.dtype)
        onehot = jax.nn.one_hot(top_idx, N_EXPERTS, dtype=x.dtype)
        prob = jnp.einsum('tk,tke->te', rw, onehot)
        prob = jnp.trunc(prob)
        h = _sq_relu(jnp.einsum('td,edf->tef', xf, W1))
        y = jnp.einsum('tef,efd->ted', h, W2)
        out_routed = jnp.einsum('ted,te->td', y, prob)
        return (out_shared + out_routed).reshape(shape)

    def _L1_xattn_ref(query_input, source_input, bias, wq, wk, wv, wo):
        import jax, jax.numpy as jnp
        import numpy as np
        HIDDEN = 128
        HEADS = 16
        HEAD_DIM = HIDDEN // HEADS
        B, F, T = (2, 256, 256)
        q = jnp.einsum('bfd,dnh->bfnh', query_input, wq)
        k = jnp.einsum('btd,dnh->btnh', source_input, wk)
        v = jnp.einsum('btd,dnh->btnh', source_input, wv)
        q = q * HEAD_DIM ** (-0.5)
        logits = jnp.einsum('btnh,bfnh->bnft', k, q)
        logits = logits + bias
        weights = jax.nn.softmax(logits, axis=-1)
        attn = jnp.einsum('bnft,btnh->bfnh', weights, v)
        return jnp.einsum('bfnh,nhd->bfd', attn, wo)

    def _L1_ffn_ref(x, q_w, k_w, v_w, o_w, sel_v_w, sel_o_w, route_scale):
        import jax, jax.numpy as jnp
        import numpy as np
        B, S, D = (2, 256, 128)
        H, E, P, K = (8, 8, 128, 2)
        SCALE = 1.0 / np.sqrt(P)

        def _get_sel_gate(x, w, route_scale):
            logits = jnp.einsum('bsd,ed->bse', x, w).astype(jnp.float32)
            raw = logits.reshape(x.shape[0], x.shape[1], H, E)
            probs = jax.nn.sigmoid(raw)
            vals, idx = jax.lax.top_k(probs, K)
            vals = vals / jnp.clip(vals.sum(-1, keepdims=True), 1e-09)
            vals = vals * route_scale
            gate = (jax.nn.one_hot(idx, E, dtype=vals.dtype) * vals[..., None]).sum(-2)
            return gate
        rs = route_scale[0]
        gate_v = _get_sel_gate(x, sel_v_w, rs)
        gate_o = _get_sel_gate(x, sel_o_w, rs)
        q = jnp.einsum('bsd,hpd->bhsp', x, q_w.reshape(H, P, D))
        k = jnp.einsum('bsd,hpd->bhsp', x, k_w.reshape(H, P, D))
        xv = jnp.einsum('bsd,hedp->bshep', x, v_w.reshape(H, E, D, P))
        v = jnp.einsum('bshep,bshe->bhsp', xv, gate_v)
        att = jax.nn.softmax(jnp.einsum('bhqp,bhkp->bhqk', q, k) * SCALE, axis=-1)
        ctx = jnp.einsum('bhqk,bhkp->bqhp', att, v)
        weighted = ctx[:, :, :, None, :] * gate_o[..., None]
        out = jnp.einsum('bshep,hepd->bsd', weighted, o_w.reshape(H, E, P, D))
        return out
    x = x + _L0_xattn_ref(_layernorm(x, axis=-1), ctx_1024, ctx_1024, mask_BxS2_if1, L0_xattn_Wq, L0_xattn_bq, L0_xattn_Wk, L0_xattn_bk, L0_xattn_Wv, L0_xattn_bv, L0_xattn_Wo, L0_xattn_bo)
    x = x + _L0_ffn_ref(_layernorm(x, axis=-1), L0_ffn_Ws1, L0_ffn_Ws2, L0_ffn_W1, L0_ffn_W2, L0_ffn_Wr)
    x = x + _L1_xattn_ref(_layernorm(x, axis=-1), ctx_1024, mask_Bx1xSxS2_ff0, L1_xattn_wq, L1_xattn_wk, L1_xattn_wv, L1_xattn_wo)
    x = x + _L1_ffn_ref(_layernorm(x, axis=-1), L1_ffn_q_w, L1_ffn_k_w, L1_ffn_v_w, L1_ffn_o_w, L1_ffn_sel_v_w, L1_ffn_sel_o_w, L1_ffn_route_scale)
    return x

_drawn_inputs = setup_inputs


def setup_inputs(seed=0):
    import zlib

    import numpy as np

    out = dict(_drawn_inputs(seed))
    spreads = {'L0_xattn_bq': (0.0, 2.0),
     'L0_xattn_bk': (0.0, 0.8),
     'L0_xattn_bv': (0.0, 0.1),
     'L0_xattn_bo': (0.0, 0.1)}
    factors = {'L0_xattn_Wq': 8.0, 'L0_xattn_Wk': 8.0, 'L0_ffn_Ws1': 3.891, 'L0_ffn_Ws2': 3.788}
    for name, (base, spread) in spreads.items():
        noise = np.random.default_rng([zlib.crc32(name.encode()), seed]).standard_normal(out[name].shape)
        drawn = base * np.exp(spread * noise) if base else spread * noise
        out[name] = jnp.asarray(drawn.astype(out[name].dtype))
    for name, factor in factors.items():
        out[name] = (out[name] * factor).astype(out[name].dtype)
    return out
```

```python
from contextlib import ExitStack

import concourse.bass as bass
from concourse import mybir

F32 = mybir.dt.float32
F32R = mybir.dt.float32r
BF16 = mybir.dt.bfloat16
I32 = mybir.dt.int32
ALU = mybir.AluOpType
ACT = mybir.ActivationFunctionType
AX_X = mybir.AxisListType.X

P = 128
SLOT = 32
MASKED = -1.0e30
EPS = 1e-5


class Step:

    def __init__(self, fn, args, kw, after, sem, by):
        self.fn, self.args, self.kw, self.after, self.sem, self.by = fn, args, kw, after, sem, by
        self.signals = by > 1
        self.count = 0


class Engine:

    def __init__(self, eng):
        self.eng, self.queue = eng, []

    def count(self, totals):
        for s in self.queue:
            if s.signals:
                totals[s.sem.name] = totals.get(s.sem.name, 0) + s.by
                s.count = totals[s.sem.name]

    def emit(self):
        seen = {}
        for s in self.queue:
            for w in s.after:
                if seen.get(w.sem.name, 0) < w.count:
                    self.eng.wait_ge(w.sem, w.count)
                    seen[w.sem.name] = w.count
            ins = s.fn(*s.args, **s.kw)
            if s.signals:
                ins.then_inc(s.sem, s.by)


class Stage:

    def __init__(self, sems):
        self.sems, self.pieces = sems, [[]]

    def put(self, engine, fn, *args, after=(), sem=None, by=1, **kw):
        for w in after:
            w.signals = True
        s = Step(fn, args, kw, list(after), sem or self.sems[engine], by)
        self.pieces[-1].append((engine, s))
        return s

    def cut(self):
        self.pieces.append([])


def interleave(stages, engines):
    order = []
    for n, st in enumerate(stages):
        k = len(st.pieces)
        order += [((i + 0.5) / k, n, i) for i in range(k)]
    for _, n, i in sorted(order):
        for engine, s in stages[n].pieces[i]:
            engines[engine].queue.append(s)


def program(nc, x_in, ctx_in, mask_in, bias_in, Wq0, bq0, Wk0, bk0, Wv0, bv0, Wo0, bo0,
            Ws1, Ws2, W1, W2, Wr, wq1, wk1, wv1, wo1, q_w, k_w, v_w, o_w, selv_w, selo_w, rscale,
            out):
    B, S, D = x_in.shape
    assert S == P and D == P
    NH, HD = wq1.shape[1], wq1.shape[2]
    NJ = P // SLOT
    NT = NH // NJ
    E0, F0 = W1.shape[0], W1.shape[2]
    NPAIR = E0 * F0 // P
    NE = 8
    H1 = v_w.shape[0] // NE
    G1 = H1 * NE
    SCALE0 = float(HD) ** -0.5
    SCALE1 = float(P) ** -0.5
    MROW0, ONE_PART = HD, 2
    MROW1 = 3 * HD

    with ExitStack() as ctx:
        def sb(name, shape, dt=F32):
            return ctx.enter_context(nc.sbuf_tensor(name, shape, dt))

        def sem(name):
            return ctx.enter_context(nc.semaphore(name))

        psA = ctx.enter_context(nc.psum_tensor("psA", [P, 2, 512], F32))
        psB = ctx.enter_context(nc.psum_tensor("psB", [P, 2, 512], F32))
        psC = ctx.enter_context(nc.psum_tensor("psC", [P, 2, 1024], F32))

        ident = sb("ident", [P, P])
        ident_r = sb("ident_r", [P, P], F32R)
        ident_b = sb("ident_b", [P, P], BF16)
        causal = sb("causal", [P, P])
        causalT = sb("causalT", [P, P])
        ones_col = sb("ones_col", [P, 1])
        minus_half = sb("minus_half", [P, 1])
        pick = sb("pick", [H1, H1, P], F32R)
        earlier = sb("earlier", [P, NE])
        WqS0 = sb("WqS0", [P, NH, SLOT], BF16)
        WkS0 = sb("WkS0", [P, NH, SLOT], BF16)
        Wv0b = sb("Wv0b", [P, P], BF16)
        Wo0b = sb("Wo0b", [P, P], BF16)
        bqS = sb("bqS", [P, NT], BF16)
        bkS = sb("bkS", [P, NT], BF16)
        bvb = sb("bvb", [P, P], BF16)
        bob = sb("bob", [P, P], BF16)
        Ws1s = sb("Ws1s", [P, F0])
        Ws2s = sb("Ws2s", [F0, P])
        W1s = sb("W1s", [P, E0, F0])
        W2s = sb("W2s", [P, NPAIR, P])
        Wrs = sb("Wrs", [P, E0])
        WqS1 = sb("WqS1", [P, NH, SLOT])
        WkS1 = sb("WkS1", [P, NH, SLOT])
        Wv1s = sb("Wv1s", [P, P])
        Wo1s = sb("Wo1s", [P, P])
        one_row = sb("one_row", [P, 1])
        less_q = sb("less_q", [P, 1])
        less_k = sb("less_k", [P, 1])
        selT = sb("selT", [P, 2 * G1])
        rs = sb("rs", [P, 1])
        Mh = sb("Mh", [P, H1, P], F32R)
        Ml = sb("Ml", [P, H1, P], F32R)
        Vh = sb("Vh", [P, G1, P], F32R)
        Vl = sb("Vl", [P, G1, P], BF16)
        Oh = sb("Oh", [P, G1, P], F32R)
        Ol = sb("Ol", [P, G1, P], BF16)
        raw = sb("raw", [P, 2, 1024])
        pick_f = raw[0:H1, 1, :].rearrange("p (h s) -> p h s", h=H1)
        prob_rows = sb("prob_rows", [P, 1])

        x_sb = sb("x_sb", [P, 2, P])
        ctx_sb = sb("ctx_sb", [P, 2, P])
        mrow_i = sb("mrow_i", [P, 2, P], I32)
        mcol_i = sb("mcol_i", [P, 2, 1], I32)
        bias_sb = sb("bias_sb", [P, 2, P])
        ctxT = sb("ctxT", [P, 2, P])
        x2 = sb("x2", [P, 2, P])
        x3 = sb("x3", [P, 2, P])
        res = sb("res", [P, 2, P])

        stA = sb("stA", [P, 6])
        mvA = sb("mvA", [P, 2])
        rsA = sb("rsA", [P, 1])
        xnbA = sb("xnbA", [P, P], BF16)
        xTbA = sb("xTbA", [P, P], BF16)
        ctxTb = sb("ctxTb", [P, P], BF16)
        maskq = sb("maskq", [P, P], BF16)
        maskk = sb("maskk", [P, P], BF16)
        keyrow = sb("keyrow", [P, P])
        keycol = sb("keycol", [P, 1])
        Qb = sb("Qb", [P, NT, P], BF16)
        Kb = sb("Kb", [P, NT, P], BF16)
        Qs = sb("Qs", [P, NT, P], BF16)
        Ks = sb("Ks", [P, NT, P], BF16)
        Q2 = sb("Q2", [P, NT, P], BF16)
        Vb = sb("Vb", [P, P], BF16)
        Vb2 = sb("Vb2", [P, P], BF16)
        Vaug = sb("Vaug", [P, NH, HD + 1])
        nmA = sb("nmA", [P, NT, NJ])
        MtA = sb("MtA", [P, NT, NJ, SLOT], BF16)
        PTA = sb("PTA", [P, 2, NT, P])
        rdA = sb("rdA", [P, NH])
        atb = sb("atb", [P, NH, HD], BF16)
        atTb = sb("atTb", [P, P], BF16)
        obA = sb("obA", [P, P], BF16)
        ob2 = sb("ob2", [P, P], BF16)
        x1 = sb("x1", [P, P])
        xnA = sb("xnA", [P, P])
        xTA = sb("xTA", [P, P])
        lg = sb("lg", [P, E0])
        top8 = sb("top8", [P, 8])
        gap = sb("gap", [P, 1])
        egap = sb("egap", [P, 1])
        sure = sb("sure", [P, 1])
        prob = sb("prob", [P, E0])
        hg = PTA[:, 0].rearrange("p t s -> p (t s)").rearrange("p (e f) -> p e f", e=E0)
        hT = PTA[:, 1]
        hs = sb("hs", [F0, P])
        hs2 = sb("hs2", [F0, P])

        stB = sb("stB", [P, 6])
        mvB = sb("mvB", [P, 2])
        rsB = sb("rsB", [P, 1])
        xnB = sb("xnB", [P, P])
        xTB = sb("xTB", [P, P])
        bh = sb("bh", [P, P], F32R)
        bl = sb("bl", [P, P], F32R)
        Qh1 = sb("Qh1", [P, NT, P])
        Qs1 = sb("Qs1", [P, NT, P], F32R)
        Ks1 = sb("Ks1", [P, NT, P], F32R)
        Q21 = sb("Q21", [P, NT, P], F32R)
        Vaug1 = sb("Vaug1", [P, NH, HD + 1])
        nmB = sb("nmB", [P, NT, NJ])
        MtB = sb("MtB", [P, NT, NJ, SLOT], F32R)
        PTB = sb("PTB", [P, 2, NT, P])
        rdB = sb("rdB", [P, NH])
        atB = sb("atB", [P, NH, HD])
        atTB = sb("atTB", [P, P])

        stC = sb("stC", [P, 6])
        mvC = sb("mvC", [P, 2])
        rsC = sb("rsC", [P, 1])
        xnC = sb("xnC", [P, P])
        xTC = sb("xTC", [P, P])
        xTh = sb("xTh", [P, P], F32R)
        xTl = sb("xTl", [P, P], F32R)
        xTb = sb("xTb", [P, P], BF16)
        yh = sb("yh", [P, H1, P], F32R)
        yl = sb("yl", [P, H1, P], F32R)
        nmC = sb("nmC", [P, P], F32R)
        nmT = sb("nmT", [P, P], F32R)
        PTC = sb("PTC", [P, H1, P])
        rdC = sb("rdC", [P, H1])
        v_sb = sb("v_sb", [P, H1, P])
        ch, cl, cb_ = yh, yl, sb("cb", [P, H1, P], BF16)
        gp = sb("gp", [P, 2 * H1, NE])
        gt = sb("gt", [P, 2 * H1, NE])
        first = sb("first", [P, 2 * H1, NE])
        second = sb("second", [P, 2 * H1, NE])
        gp2 = sb("gp2", [P, 2 * H1, NE])
        m1 = sb("m1", [P, 2 * H1])
        m2 = sb("m2", [P, 2 * H1])
        r1 = sb("r1", [P, 2 * H1])
        gsum = sb("gsum", [P, 2 * H1])
        gate = sb("gate", [P, 2 * H1, NE])
        gateO = sb("gateO", [P, H1, NE])
        TE = sb("TE", [P, 2, NE // 2, P])
        DE = TE
        FE = sb("FE", [P, 2, P])
        accO = sb("accO", [P, 2, P])

        def counters(tag):
            return {e: sem(f"{e}_{tag}") for e in ("pe", "act", "dve", "pool", "sp")}

        semW, semA, semB, semC = (counters(t) for t in ("setup", "A", "B", "C"))
        s_in = [sem(f"in{k}") for k in range(2)]
        s_bias = [sem(f"bias{k}") for k in range(2)]
        s_out = [sem(f"out{k}") for k in range(2)]
        s_small = sem("small_weights")
        s_raw = [sem(f"raw{k}") for k in range(2)]

        engines = {"pe": Engine(nc.tensor), "act": Engine(nc.scalar), "dve": Engine(nc.vector),
                   "pool": Engine(nc.gpsimd), "sp": Engine(nc.sync)}
        T, V, A, G, SY = nc.tensor, nc.vector, nc.scalar, nc.gpsimd, nc.sync

        def mm(st, o, l, r, start, stop, after=()):
            return st.put("pe", T.matmul, o, l, r, start=start, stop=stop, after=after)

        def over_heads(ap2, n):
            return ap2.unsqueeze(1).to_broadcast([ap2.shape[0], n, ap2.shape[1]])

        def along(ap2, n):
            return ap2.unsqueeze(2).to_broadcast([ap2.shape[0], ap2.shape[1], n])

        def f(ap):
            return ap.bitcast(F32)

        W = Stage(semW)

        def load(dst, src, s, after=()):
            return W.put("sp", SY.dma_start, dst, src, sem=s, by=16, after=after)

        def wide(v, n=P):
            return v.rearrange("(a n) -> a n", a=1).to_broadcast([n, v.shape[0]])

        zi = W.put("pool", G.memset, ident[:], 0.0)
        zi2 = W.put("pool", G.affine_select, out=ident[:], in_=ident[:], compare_op=ALU.not_equal,
                    fill=1.0, base=0, pattern=[[-1, P]], channel_multiplier=1, after=[zi])
        id_r = W.put("pool", G.tensor_copy, ident_r[:], ident[:], after=[zi2])
        id_b = W.put("pool", G.tensor_copy, ident_b[:], ident[:], after=[zi2])
        zc = W.put("pool", G.memset, causal[:], 0.0)
        zct = W.put("pool", G.memset, causalT[:], 0.0)
        cq = W.put("pool", G.affine_select, out=causal[:], in_=causal[:], compare_op=ALU.is_ge,
                   fill=MASKED, base=0, pattern=[[-1, P]], channel_multiplier=1, after=[zc])
        ck = W.put("pool", G.affine_select, out=causalT[:], in_=causalT[:], compare_op=ALU.is_ge,
                   fill=MASKED, base=0, pattern=[[1, P]], channel_multiplier=-1, after=[zct])
        zp = W.put("pool", G.memset, pick_f[:], 0.0)
        pk = W.put("pool", G.affine_select, out=pick_f[:], in_=pick_f[:], compare_op=ALU.not_equal,
                   fill=1.0, base=0, pattern=[[-1, H1], [0, P]], channel_multiplier=1, after=[zp])
        pk = W.put("pool", G.tensor_copy, pick[:], pick_f[:], after=[pk])
        c1 = W.put("pool", G.memset, ones_col[:], 1.0)
        c2 = W.put("pool", G.memset, minus_half[:], -0.5)
        for e in range(NE):
            c3 = W.put("pool", G.memset, earlier[:, e:e + 1], float(NE - e))
        z0 = W.put("pool", G.memset, WqS0[:], 0.0)
        z1 = W.put("pool", G.memset, WkS0[:], 0.0)
        z2 = W.put("pool", G.memset, WqS1[:], 0.0)
        z3 = W.put("pool", G.memset, WkS1[:], 0.0)
        zq = W.put("dve", V.memset, MtA[:], 0.0)
        zr = W.put("dve", V.memset, MtB[:].bitcast(F32), 0.0)
        zn = W.put("dve", V.memset, nmC[:].bitcast(F32), 0.0)
        zv = W.put("dve", V.memset, Vaug[:, :, HD:HD + 1], 1.0)
        zv1 = W.put("dve", V.memset, Vaug1[:, :, HD:HD + 1], 1.0)

        rows3 = PTB[0:1, 0].rearrange("p t (j s) -> p t j s", j=NJ)
        w0 = W.put("dve", V.memset, rows3, 0.0)
        wa = W.put("dve", V.memset, rows3[:, 0, :, MROW1:MROW1 + 2], 1.0, after=[w0])
        wb = W.put("dve", V.memset, rows3[:, 1, :, 2 * HD:3 * HD], -1.0, after=[w0])
        wc = W.put("dve", V.memset, rows3[:, 2, :, HD:2 * HD], -1.0, after=[w0])
        wd = W.put("dve", V.memset, rows3[:, 2, :, MROW1:MROW1 + 2], 1.0, after=[w0])
        we = W.put("dve", V.memset, rows3[:, 3, :, MROW0:MROW0 + 2], 1.0, after=[w0])
        bias_rows = PTB[0:NT, 1, 0:2].rearrange("p n (j s) -> p n j s", j=NJ)
        zb = W.put("dve", V.memset, bias_rows, 0.0)
        wq0_raw = raw[:, 0, 0:P]
        wk0_raw = raw[:, 0, P:2 * P]
        wv0_raw = raw[:, 0, 2 * P:3 * P]
        wo0_raw = raw[:, 0, 3 * P:4 * P]
        wq1_raw = raw[:, 0, 4 * P:5 * P]
        wk1_raw = raw[:, 0, 5 * P:6 * P]
        bv_raw = raw[:, 0, 6 * P:7 * P]
        bo_raw = raw[:, 0, 7 * P:8 * P]
        sel_raw = raw[:, 1, 0:P]
        small = []
        for dst, src in ((wq0_raw, Wq0), (wk0_raw, Wk0), (wv0_raw, Wv0), (wo0_raw, Wo0),
                         (wq1_raw, wq1.rearrange("d n h -> d (n h)")),
                         (wk1_raw, wk1.rearrange("d n h -> d (n h)")),
                         (bv_raw, wide(bv0)), (bo_raw, wide(bo0)),
                         (sel_raw[0:G1, :], selv_w), (sel_raw[G1:2 * G1, :], selo_w),
                         (rs[:], wide(rscale)),
                         (Ws1s[:], Ws1), (Ws2s[:], Ws2), (W1s[:], W1.rearrange("e d f -> d e f")),
                         (W2s[:], W2.rearrange("(a e) f d -> (e f) a d", a=NPAIR)),
                         (Wrs[:], Wr),
                         (Wv1s[:], wv1.rearrange("d n h -> d (n h)")),
                         (Wo1s[:], wo1.rearrange("n h d -> (n h) d"))):
            small.append(load(dst, src, s_small, after=[pk]))
        for t in range(NT):
            for n, v in enumerate((bq0, bk0)):
                small.append(load(bias_rows[t:t + 1, n, :, 0:HD],
                                  v[t * NJ * HD:(t + 1) * NJ * HD].rearrange("(a j d) -> a j d", a=1, d=HD),
                                  s_small, after=[zb]))
        sm = small[-1]

        sc = W.put("act", A.activation, WqS0[:, :, 0:HD], wq0_raw.rearrange("p (n d) -> p n d", d=HD),
                   ACT.Copy, after=[sm, z0])
        sc = W.put("act", A.activation, WkS0[:, :, 0:HD], wk0_raw.rearrange("p (n d) -> p n d", d=HD),
                   ACT.Copy, after=[z1])
        sc = W.put("act", A.activation, Wv0b[:], wv0_raw, ACT.Copy)
        sc = W.put("act", A.activation, Wo0b[:], wo0_raw, ACT.Copy)
        sc = W.put("act", A.activation, bvb[:], bv_raw, ACT.Copy)
        sc = W.put("act", A.activation, bob[:], bo_raw, ACT.Copy)
        for r in range(3):
            sc = W.put("act", A.mul, WqS1[:, :, r * HD:(r + 1) * HD],
                       wq1_raw.rearrange("p (n d) -> p n d", d=HD), SCALE0, after=[z2])
            sc = W.put("act", A.activation, WkS1[:, :, r * HD:(r + 1) * HD],
                       wk1_raw.rearrange("p (n d) -> p n d", d=HD), ACT.Copy, after=[z3])
        scaled = sc
        for n in range(4):
            tr = mm(W, psA[:, 0, n:n + 1], rows3[:, n].rearrange("a j s -> a (j s)"), ones_col[0:1, :],
                    True, True, after=[wa, wb, wc, wd, we, c1])
        tb = mm(W, psA[:, 0, 8:8 + NT], bias_rows[:, 0].rearrange("t j s -> t (j s)"), ident[0:NT, 0:NT],
                True, True, after=[sm, zb, zi2])
        tb = mm(W, psA[:, 0, 16:16 + NT], bias_rows[:, 1].rearrange("t j s -> t (j s)"), ident[0:NT, 0:NT],
                True, True)
        d1 = W.put("dve", V.tensor_copy, one_row[:], psA[:, 0, 0:1], after=[tb])
        d1 = W.put("dve", V.tensor_copy, less_q[:], psA[:, 0, 1:2])
        d1 = W.put("dve", V.tensor_copy, less_k[:], psA[:, 0, 2:3])
        d0 = W.put("dve", V.tensor_copy, prob_rows[:], psA[:, 0, 3:4])
        d1 = W.put("dve", V.tensor_copy, bqS[:], psA[:, 0, 8:8 + NT])
        d1 = W.put("dve", V.tensor_scalar, bkS[:], psA[:, 0, 16:16 + NT], prob_rows[:], None, ALU.add,
                   after=[d0])
        ts = W.put("pe", T.transpose, psA[:, 1, 0:P], sel_raw, ident[:], after=[sm, zi2])
        small_done = W.put("dve", V.tensor_copy, selT[:], psA[:, 1, 0:P], after=[ts])

        W.cut()
        qload = load(raw[:, 0, :].rearrange("p (h d) -> p h d", h=H1),
                     q_w.rearrange("(h p) d -> p h d", p=P), s_raw[0], after=[scaled])
        kload = load(raw[:, 1, :].rearrange("p (h d) -> p h d", h=H1),
                     k_w.rearrange("(h p) d -> p h d", p=P), s_raw[1], after=[ts])
        for h in range(H1):
            mh = mm(W, psC[:, 0, h * P:(h + 1) * P], raw[:, 0, h * P:(h + 1) * P],
                    raw[:, 1, h * P:(h + 1) * P], True, True, after=[qload, kload])
        hi = W.put("act", A.activation, Mh[:].rearrange("p h d -> p (h d)"), psC[:, 0, :], ACT.Copy,
                   after=[mh])
        Mdone = W.put("dve", V.tensor_tensor, Ml[:].rearrange("p h d -> p (h d)"), psC[:, 0, :],
                      f(Mh[:]).rearrange("p h d -> p (h d)"), ALU.subtract, after=[hi])
        last_read = [Mdone, Mdone]
        cut_done = {}
        n = 0
        for name, src, hi_sb, lo_sb in (("v", v_w, Vh, Vl), ("o", o_w, Oh, Ol)):
            for h in range(H1):
                k = n % 2
                got = load(raw[:, k, :].rearrange("p (e n) -> p e n", e=NE),
                           src[h * NE:(h + 1) * NE].rearrange("e p n -> p e n"), s_raw[k],
                           after=[last_read[k]])
                hsl = hi_sb[:, h * NE:(h + 1) * NE, :].rearrange("p e n -> p (e n)")
                lsl = lo_sb[:, h * NE:(h + 1) * NE, :].rearrange("p e n -> p (e n)")
                hi = W.put("act", A.activation, hsl, raw[:, k, :], ACT.Copy, after=[got])
                lo = W.put("dve", V.tensor_tensor, lsl, raw[:, k, :], f(hsl), ALU.subtract, after=[hi, got])
                last_read[k] = lo
                cut_done[name, h] = lo
                n += 1
                W.cut()

        def layernorm(st, x, stats, mv, rstd, dst, after):
            a = st.put("dve", V.bn_stats, stats[:], x, after=after)
            a = st.put("dve", V.bn_aggr, mv[:], stats[:], after=[a])
            st.cut()
            p = st.put("pool", G.tensor_scalar, rstd[:], mv[:, 1:2], EPS, None, ALU.add, after=[a, c2])
            p = st.put("pool", G.tensor_tensor, rstd[:], rstd[:], minus_half[:], ALU.pow, after=[p])
            st.cut()
            return st.put("dve", V.tensor_scalar, dst[:], x, mv[:, 0:1], rstd[:], ALU.subtract, ALU.mult,
                          after=[p])

        state = {}

        def since(*keys):
            return [state[k] for k in keys if k in state]

        def loads(b):
            st = Stage(semW)
            k = b % 2
            for key, dst, src in (("x1", x_sb[:, k], x_in[b]), ("ctx", ctx_sb[:, k], ctx_in[b]),
                                  ("mask", mrow_i[:, k], wide(mask_in[b])),
                                  ("mask", mcol_i[:, k], mask_in[b].rearrange("(s a) -> s a", a=1))):
                state["in", b] = st.put("sp", SY.dma_start, dst, src, sem=s_in[k], by=16,
                                        after=since((key, b - 2)))
            return st

        def load_bias(b):
            st = Stage(semW)
            state["inbias", b] = st.put("sp", SY.dma_start, bias_sb[:, b % 2], bias_in[b, 0],
                                        sem=s_bias[b % 2], by=16, after=since(("bias", b - 2)))
            return st

        def attend(st, ps, free, Qslot, Kslot, Qwithmax, Mt, nm, PT, Vp, at, rden, mask_q, mask_k, mrow,
                   scale, ident_mm, ready, vready):
            def scores(j, bank, Ql, Kr, pairs, after):
                o = ps[:, bank, :].rearrange("p (t s) -> p t s", t=NT)
                rows_j = slice(SLOT * j, SLOT * (j + 1))
                for n, (l, r) in enumerate(pairs):
                    mm(st, o, l, r, n == 0, False, after=after)
                for t in range(NT):
                    last = mm(st, o[:, t, :], Ql[rows_j, t, :], Kr[rows_j, t, :], False, t == NT - 1,
                              after=after)
                return last

            for j in range(NJ):
                bank = j % 2
                s = scores(j, bank, Qslot, Kslot, mask_q, [*ready, *free[bank]])
                m = st.put("dve", V.tensor_reduce, nm[:, :, j], ps[:, bank, :].rearrange("p (t s) -> p t s", t=NT),
                           AX_X, ALU.max, negate=True, after=[s])
                free[bank] = [m]
                st.cut()
            nmv = nm[:].rearrange("p t j -> p t j")
            hi = st.put("dve", V.tensor_copy, Mt[:, :, :, mrow], nmv, after=[m])
            hv = Mt[:, :, :, mrow]
            lo = st.put("dve", V.tensor_tensor, Mt[:, :, :, mrow + 1], nmv,
                        f(hv) if Mt.dtype == F32R else hv, ALU.subtract, after=[hi])
            st.cut()
            for t in range(NT):
                tp = mm(st, ps[:, 0, t * P:(t + 1) * P], Mt[:, t].rearrange("p j s -> p (j s)"), ident_mm,
                        True, True, after=[lo, *free[0]])
            st.cut()
            q = f(Qslot[:]) if Qslot.dtype == F32R else Qslot[:]
            q2 = st.put("dve", V.tensor_tensor, Qwithmax[:], ps[:, 0, :].rearrange("p (t s) -> p t s", t=NT),
                        q, ALU.add, after=[tp])
            free[0] = [q2]
            st.cut()
            o = ps[:, 0, 0:NH * (HD + 1)].rearrange("p (n w) -> p n w", n=NH)
            used = [[], []]
            for j in range(NJ):
                s = scores(j, 1, Kslot, Qwithmax, mask_k, [q2, *free[1]])
                e = st.put("act", A.activation, PT[:, j % 2].rearrange("p t s -> p (t s)"), ps[:, 1, :],
                           ACT.Exp, scale=scale, after=[s, *used[j % 2]])
                free[1] = [e]
                st.cut()
                for t in range(NT):
                    pv = mm(st, o[:, NJ * t + j, :], PT[:, j % 2, t, :], Vp[:, NJ * t + j, :], True, True,
                            after=[e, vready, *free[0]])
                used[j % 2] = [pv]
                st.cut()
            r = st.put("dve", V.reciprocal, rden[:], o[:, :, HD], after=[pv])
            a = st.put("dve", V.tensor_tensor, at[:], o[:, :, 0:HD], along(rden[:], HD), ALU.mult, after=[r])
            free[0] = [a]
            st.cut()
            return a

        freeA = {0: [small_done], 1: [small_done]}
        freeB = {0: [], 1: []}
        freeC = {0: [Mdone], 1: [Mdone]}

        def stage_a(b):
            st = Stage(semA)
            k = b % 2
            x = x_sb[:, k]
            loaded = state["in", b]
            mk = st.put("pool", G.tensor_scalar, keyrow[:], mrow_i[:, k], 0, MASKED, ALU.is_le, ALU.mult,
                        after=[loaded, cq, ck, *since(("maskused", b - 1))])
            mk1 = st.put("pool", G.tensor_scalar, keycol[:], mcol_i[:, k], 0, MASKED, ALU.is_le, ALU.mult)
            mk2 = st.put("pool", G.tensor_tensor, maskq[:], keyrow[:], causal[:], ALU.add, after=[mk])
            masks = st.put("pool", G.tensor_scalar, maskk[:], causalT[:], keycol[:], None, ALU.add,
                           after=[mk1])
            state["mask", b] = mk1
            n = layernorm(st, x, stA, mvA, rsA, xnbA, [loaded])
            psb = psA[:, 0, 0:64].bitcast(BF16)
            st.cut()
            tp = st.put("pe", T.transpose, psb, xnbA[:], ident_b[:], after=[n, id_b, *freeA[0]])
            tc = st.put("pe", T.transpose, psA[:, 1, 0:P], ctx_sb[:, k], ident[:], after=[loaded, zi2, *freeA[1]])
            state["ctx", b] = tc
            st.cut()
            c = st.put("act", A.activation, xTbA[:], psb, ACT.Copy, after=[tp])
            cc = st.put("act", A.activation, ctxT[:, k], psA[:, 1, 0:P], ACT.Copy,
                        after=[tc, *since(("ctxTused", b - 2))])
            cb = st.put("act", A.activation, ctxTb[:], psA[:, 1, 0:P], ACT.Copy)
            state["ctxT", b] = cc
            st.cut()
            wq = WqS0[:].rearrange("p n s -> p (n s)")
            wk = WkS0[:].rearrange("p n s -> p (n s)")
            for t in range(NT):
                q = mm(st, psA[:, 0, t * P:(t + 1) * P], wq[:, t * P:(t + 1) * P], xTbA[:], True, True,
                       after=[c, scaled])
            for t in range(NT):
                kk = mm(st, psA[:, 1, t * P:(t + 1) * P], wk[:, t * P:(t + 1) * P], ctxTb[:], True, True,
                        after=[cb])
            st.cut()
            qb = st.put("act", A.activation, Qb[:].rearrange("p t s -> p (t s)"), psA[:, 0, :], ACT.Copy,
                        after=[q])
            kb = st.put("act", A.activation, Kb[:].rearrange("p t s -> p (t s)"), psA[:, 1, :], ACT.Copy,
                        after=[kk])
            st.cut()
            v = mm(st, psA[:, 0, 0:P], ctxTb[:], Wv0b[:], True, True, after=[qb])
            vb = st.put("act", A.activation, Vb[:], psA[:, 0, 0:P], ACT.Copy, after=[v])
            st.cut()
            qs = st.put("pool", G.tensor_tensor, Qs[:], Qb[:], along(bqS[:], P), ALU.add, after=[qb, small_done])
            ks = st.put("pool", G.tensor_tensor, Ks[:], Kb[:], along(bkS[:], P), ALU.add, after=[kb])
            vb2 = st.put("pool", G.tensor_tensor, Vb2[:], Vb[:], bvb[:], ALU.add, after=[vb, scaled])
            va = st.put("pool", G.tensor_copy, Vaug[:, :, 0:HD], Vb2[:].rearrange("p (n d) -> p n d", d=HD),
                        after=[vb2, zv])
            st.cut()
            free = {0: [vb], 1: [kb]}
            a = attend(st, psA, free, Qs, Ks, Q2, MtA, nmA, PTA, Vaug, atb, rdA,
                       [(ident_b[:], over_heads(maskq[:], NT))], [(ident_b[:], over_heads(maskk[:], NT))],
                       MROW0, SCALE0, ident_b[:], [ks, masks, zq], va)
            tp = st.put("pe", T.transpose, psA[:, 1, 0:64].bitcast(BF16), atb[:].rearrange("p n d -> p (n d)"),
                        ident_b[:], after=[a, *free[1]])
            state["maskused", b] = tp
            c = st.put("act", A.activation, atTb[:], psA[:, 1, 0:64].bitcast(BF16), ACT.Copy, after=[tp])
            st.cut()
            o = mm(st, psA[:, 0, 0:P], atTb[:], Wo0b[:], True, True, after=[c, *free[0]])
            ob = st.put("act", A.activation, obA[:], psA[:, 0, 0:P], ACT.Copy, after=[o])
            st.cut()
            o2 = st.put("pool", G.tensor_tensor, ob2[:], obA[:], bob[:], ALU.add, after=[ob])
            xx = st.put("pool", G.tensor_tensor, x1[:], x, ob2[:], ALU.add, after=[o2])
            state["x1", b] = xx
            st.cut()
            n = layernorm(st, x1[:], stA, mvA, rsA, xnA, [xx])
            st.cut()
            tp = st.put("pe", T.transpose, psA[:, 1, 0:P], xnA[:], ident[:], after=[n])
            xt = st.put("act", A.activation, xTA[:], psA[:, 1, 0:P], ACT.Copy, after=[tp])
            st.cut()
            rl = mm(st, psA[:, 0, 0:E0], xTA[:], Wrs[:], True, True, after=[xt, sm])
            l = st.put("dve", V.tensor_copy, lg[:], psA[:, 0, 0:E0], after=[rl])
            t8 = st.put("dve", V.max, top8[:], lg[:], after=[l])
            gp_ = st.put("dve", V.tensor_tensor, gap[:], top8[:, 1:2], top8[:, 0:1], ALU.subtract, after=[t8])
            st.cut()
            hid = mm(st, psA[:, 1, :], xTA[:], W1s[:].rearrange("p e f -> p (e f)"), True, True)
            sh = mm(st, psA[0:F0, 0, 0:P], Ws1s[:], xTA[:], True, True, after=[l])
            eg = st.put("act", A.activation, egap[:], gap[:], ACT.Exp, after=[gp_])
            r_ = st.put("act", A.activation, hs[:], psA[0:F0, 0, 0:P], ACT.Relu, after=[sh])
            r2_ = st.put("act", A.activation, hs2[:], hs[:], ACT.Square, after=[r_])
            st.cut()
            su = st.put("dve", V.tensor_scalar, sure[:], egap[:], 1.0, 1.0, ALU.add, ALU.is_equal, after=[eg])
            pr = st.put("dve", V.tensor_scalar, prob[:], lg[:], top8[:, 0:1], sure[:], ALU.is_equal, ALU.mult,
                        after=[su])
            hgs = st.put("dve", V.scalar_tensor_tensor, hg, psA[:, 1, :].rearrange("p (e f) -> p e f", e=E0),
                         0.0, along(prob[:], F0), ALU.max, ALU.mult, after=[pr, hid])
            st.cut()
            hgf = hg.rearrange("p e f -> p (e f)")
            for a_ in range(NPAIR):
                tp = st.put("pe", T.transpose, psA[:, 1, a_ * P:(a_ + 1) * P], hgf[:, a_ * P:(a_ + 1) * P],
                            ident[:], after=[hgs])
            hq = st.put("act", A.activation, hT.rearrange("p a s -> p (a s)"), psA[:, 1, :], ACT.Square,
                        after=[tp])
            st.cut()
            mm(st, psA[:, 0, 0:P], hs2[:], Ws2s[:], True, False, after=[r2_])
            for a_ in range(NPAIR):
                y = mm(st, psA[:, 0, 0:P], hT[:, a_, :], W2s[:, a_, :], False, a_ == NPAIR - 1, after=[hq])
            xo = st.put("dve", V.tensor_tensor, x2[:, k], psA[:, 0, 0:P], x1[:], ALU.add,
                        after=[y, *since(("x2used", b - 2))])
            state["x2", b] = xo
            freeA[0], freeA[1] = [xo], [hq]
            return st

        def stage_b(b):
            st = Stage(semB)
            k = b % 2
            x = x2[:, k]
            loaded = state["inbias", b]
            b0 = st.put("pool", G.tensor_copy, bh[:], bias_sb[:, k], after=[loaded, *since(("biasused", b - 1))])
            b1 = st.put("pool", G.tensor_tensor, bl[:], bias_sb[:, k], f(bh[:]), ALU.subtract, after=[b0])
            state["bias", b] = b1
            n = layernorm(st, x, stB, mvB, rsB, xnB, [state["x2", b]])
            st.cut()
            tp = st.put("pe", T.transpose, psB[:, 0, 0:P], xnB[:], ident[:], after=[n, zi2, *freeB[0]])
            c = st.put("act", A.activation, xTB[:], psB[:, 0, 0:P], ACT.Copy, after=[tp])
            wq = WqS1[:].rearrange("p n s -> p (n s)")
            wk = WkS1[:].rearrange("p n s -> p (n s)")
            for t in range(NT):
                kk = mm(st, psB[:, 1, t * P:(t + 1) * P], wk[:, t * P:(t + 1) * P], ctxT[:, k], True, True,
                        after=[scaled, state["ctxT", b], *freeB[1]])
            st.cut()
            kh = st.put("act", A.activation, Qh1[:].rearrange("p t s -> p (t s)").bitcast(F32R), psB[:, 1, :],
                        ACT.Identity, bias=one_row[:], after=[kk, small_done])
            k2 = st.put("dve", V.scalar_tensor_tensor, Ks1[:].rearrange("p t s -> p (t s)"),
                        Qh1[:].rearrange("p t s -> p (t s)"), less_k[:], psB[:, 1, :], ALU.mult, ALU.add, after=[kh])
            for t in range(NT):
                q = mm(st, psB[:, 0, t * P:(t + 1) * P], wq[:, t * P:(t + 1) * P], xTB[:], True, True, after=[c])
            st.cut()
            qh = st.put("act", A.activation, Qh1[:].rearrange("p t s -> p (t s)").bitcast(F32R), psB[:, 0, :],
                        ACT.Copy, after=[q, k2])
            q2 = st.put("dve", V.scalar_tensor_tensor, Qs1[:].rearrange("p t s -> p (t s)"),
                        Qh1[:].rearrange("p t s -> p (t s)"), less_q[:], psB[:, 0, :], ALU.mult, ALU.add, after=[qh])
            st.cut()
            v = mm(st, psB[:, 1, 0:P], ctxT[:, k], Wv1s[:], True, True, after=[k2, sm])
            state["ctxTused", b] = v
            va = st.put("act", A.activation, Vaug1[:, :, 0:HD],
                        psB[:, 1, 0:P].rearrange("p (n d) -> p n d", d=HD), ACT.Copy, after=[v, zv1])
            st.cut()
            free = {0: [q2], 1: [va]}
            a = attend(st, psB, free, Qs1, Ks1, Q21, MtB, nmB, PTB, Vaug1, atB, rdB,
                       [(ident_r[:], over_heads(bh[:], NT)), (ident_r[:], over_heads(bl[:], NT))],
                       [(bh[:], over_heads(ident_r[:], NT)), (bl[:], over_heads(ident_r[:], NT))],
                       MROW1, 1.0, ident_r[:], [q2, b1, id_r, zr], va)
            tp = st.put("pe", T.transpose, psB[:, 1, 0:P], atB[:].rearrange("p n d -> p (n d)"), ident[:],
                        after=[a, *free[1]])
            state["biasused", b] = tp
            c = st.put("act", A.activation, atTB[:], psB[:, 1, 0:P], ACT.Copy, after=[tp])
            st.cut()
            o = mm(st, psB[:, 0, 0:P], atTB[:], Wo1s[:], True, True, after=[c, *free[0]])
            xo = st.put("dve", V.tensor_tensor, x3[:, k], psB[:, 0, 0:P], x, ALU.add,
                        after=[o, *since(("x3used", b - 2))])
            state["x2used", b] = xo
            state["x3", b] = xo
            freeB[0], freeB[1] = [xo], [c]
            return st

        turn = [0]

        def stage_c(b):
            st = Stage(semC)
            k = b % 2
            x = x3[:, k]

            def pair():
                p = turn[0] % 2
                turn[0] += 1
                return psC[:, p], p

            n = layernorm(st, x, stC, mvC, rsC, xnC, [state["x3", b]])
            st.cut()
            ps, p = pair()
            tp = st.put("pe", T.transpose, ps[:, 0:P], xnC[:], ident[:], after=[n, zi2, *freeC[p]])
            h_ = st.put("act", A.activation, xTh[:], ps[:, 0:P], ACT.Copy, after=[tp])
            c = st.put("act", A.activation, xTC[:], ps[:, 0:P], ACT.Copy)
            xb_ = st.put("pool", G.tensor_copy, xTb[:], xTC[:], after=[c])
            l_ = st.put("dve", V.tensor_tensor, xTl[:], ps[:, 0:P], f(xTh[:]), ALU.subtract, after=[h_, c])
            st.cut()
            gl = mm(st, ps[:, 512:512 + 2 * G1], xTC[:], selT[:], True, True, after=[c, small_done])
            st.cut()
            gpf = gp[:].rearrange("p g e -> p (g e)")
            e_ = st.put("act", A.activation, gpf, ps[:, 512:512 + 2 * G1], ACT.Exp, scale=-1.0, after=[gl])
            freeC[p] = [l_, e_]
            g = st.put("pool", G.tensor_scalar, gpf, gpf, 1.0, None, ALU.add, after=[e_])
            ps, p = pair()
            for h in range(H1):
                o = ps[:, h * P:(h + 1) * P]
                mm(st, o, Mh[:, h], xTh[:], True, False, after=[h_, Mdone, *freeC[p]])
                mm(st, o, Ml[:, h], xTh[:], False, False)
                y = mm(st, o, Mh[:, h], xTl[:], False, True, after=[l_])
                if h % 4 == 3:
                    i = h // 4
                    yhf = yh[:, 4 * i:4 * i + 4].rearrange("p h s -> p (h s)")
                    ylf = yl[:, 4 * i:4 * i + 4].rearrange("p h s -> p (h s)")
                    yy = st.put("act", A.activation, yhf, ps[:, 512 * i:512 * i + 512], ACT.Copy, after=[y])
                    st.cut()
                    yx = st.put("dve", V.tensor_tensor, ylf, ps[:, 512 * i:512 * i + 512], f(yhf), ALU.subtract,
                                after=[yy])
                    st.cut()
            freeC[p] = [yx]
            g = st.put("dve", V.reciprocal, gpf, gpf, after=[g])
            g = st.put("dve", V.tensor_reduce, m1[:], gp[:], AX_X, ALU.max, after=[g])
            st.cut()

            def first_best(src, best, dst, after):
                a = st.put("dve", V.tensor_tensor, gt[:], src[:], along(best[:], NE), ALU.is_equal, after=after)
                a = st.put("dve", V.tensor_tensor, gt[:], gt[:], over_heads(earlier[:], 2 * H1), ALU.mult,
                           after=[a, c3])
                a = st.put("dve", V.tensor_reduce, r1[:], gt[:], AX_X, ALU.max, after=[a])
                return st.put("dve", V.tensor_tensor, dst[:], gt[:], along(r1[:], NE), ALU.is_equal, after=[a])

            g = first_best(gp, m1, first, [g])
            st.cut()
            ps, p = pair()
            for h in range(H1):
                s = mm(st, ps[:, h * P:(h + 1) * P], yh[:, h], xTh[:], True, True, after=[yy, *freeC[p]])
            st.cut()
            g = st.put("dve", V.scalar_tensor_tensor, gp2[:].rearrange("p g e -> p (g e)"),
                       first[:].rearrange("p g e -> p (g e)"), -2.0, gpf, ALU.mult, ALU.add, after=[g])
            g = st.put("dve", V.tensor_reduce, m2[:], gp2[:], AX_X, ALU.max, after=[g])
            g = first_best(gp2, m2, second, [g])
            st.cut()
            nm = st.put("dve", V.tensor_reduce, nmC[:, 0:H1], ps.rearrange("p (h s) -> p h s", h=H1), AX_X,
                        ALU.max, negate=True, after=[s, zn])
            freeC[p] = [nm]
            st.cut()
            q = st.put("dve", V.tensor_tensor, gsum[:], m1[:], m2[:], ALU.add, after=[g])
            q = st.put("dve", V.tensor_scalar, gsum[:], gsum[:], 1e-9, None, ALU.max, after=[q])
            q = st.put("dve", V.reciprocal, gsum[:], gsum[:], after=[q])
            q = st.put("dve", V.tensor_scalar, gsum[:], gsum[:], rs[:], None, ALU.mult, after=[q, sm])
            q1 = st.put("dve", V.tensor_tensor, m1[:], m1[:], gsum[:], ALU.mult, after=[q])
            q2 = st.put("dve", V.tensor_tensor, m2[:], m2[:], gsum[:], ALU.mult, after=[q])
            q1 = st.put("pool", G.tensor_tensor, first[:], first[:], along(m1[:], NE), ALU.mult, after=[q2])
            q2 = st.put("pool", G.tensor_tensor, second[:], second[:], along(m2[:], NE), ALU.mult)
            gt_ = st.put("pool", G.tensor_tensor, gate[:], first[:], second[:], ALU.add, after=[q1, q2])
            st.cut()
            ps, p = pair()
            tm = mm(st, ps[:, 0:P], nmC[:], ident_r[:], True, True, after=[nm, id_r, *freeC[p]])
            tmc = st.put("act", A.activation, nmT[:], ps[:, 0:P], ACT.Copy, after=[tm])
            freeC[p] = [tmc]
            st.cut()
            ps, p = pair()
            for i in range(H1 // 4):
                o = ps[:, 512 * i:512 * i + 512]
                yhf = yh[:, 4 * i:4 * i + 4].rearrange("p h s -> p (h s)")
                ylf = yl[:, 4 * i:4 * i + 4].rearrange("p h s -> p (h s)")
                mm(st, o, xTh[:], yhf, True, False, after=[*freeC[p]])
                mm(st, o, xTh[:], ylf, False, False, after=[yx])
                mm(st, o, xTl[:], yhf, False, False)
                for h in range(4 * i, 4 * i + 4):
                    s = mm(st, ps[:, h * P:(h + 1) * P], pick[:, h, :], nmT[0:H1, :], False, h % 4 == 3,
                           after=[tmc, pk])
                ex = st.put("act", A.activation, PTC[:, 4 * i:4 * i + 4].rearrange("p h s -> p (h s)"), o,
                            ACT.Exp, scale=SCALE1, after=[s])
                st.cut()
            freeC[p] = [ex]

            parity = [0]

            def experts(lhs, w_hi, w_lo, h, g_of, gates_ready, after):
                i = parity[0] % 2
                parity[0] += 1
                ps, p = pair()
                for half in (1, 0):
                    o = ps[:, 512 * half:512 * half + 512]
                    e0 = h * NE + half * (NE // 2)
                    wh = w_hi[:, e0:e0 + NE // 2].rearrange("p e n -> p (e n)")
                    wl = w_lo[:, e0:e0 + NE // 2].rearrange("p e n -> p (e n)")
                    mm(st, o, lhs[0], wh, True, False, after=[*after, *freeC[p]])
                    mm(st, o, lhs[1], wh, False, False)
                    z = mm(st, o, lhs[2], wl, False, True)
                    if half:
                        z1_ = z
                te = []
                for e in range(NE // 2):
                    te.append(st.put("act", A.activation, TE[:, i, e], ps[:, 512 + e * P:512 + (e + 1) * P],
                                     ACT.Copy, scale=g_of(h, e + NE // 2),
                                     after=[z1_, gates_ready, *since(("fe", i))]))
                st.cut()
                for e in range(NE // 2):
                    de = st.put("dve", V.scalar_tensor_tensor, DE[:, i, e], ps[:, e * P:(e + 1) * P],
                                g_of(h, e), TE[:, i, e], ALU.mult, ALU.add,
                                after=[z, te[e], gates_ready, *since(("fe", i))])
                freeC[p] = [de, te[-1]]
                state["de", i] = de
                st.cut()
                return i, de

            for h in range(H1):
                i, de = experts((xTh[:], xTl[:], xTb[:]), Vh, Vl, h, lambda h, e: gate[:, h, e:e + 1], gt_,
                                [cut_done["v", h], xb_])
                fe = st.put("pool", G.tensor_tensor, FE[:], DE[:, i, 0:2], DE[:, i, 2:4], ALU.add,
                            after=[de, *since("FEread")])
                vv = st.put("pool", G.tensor_tensor, v_sb[:, h], FE[:, 0], FE[:, 1], ALU.add, after=[fe])
                state["fe", i], state["FEread"] = fe, vv
                st.cut()
                if h == 2:
                    ps, p = pair()
                    for hh in range(H1):
                        dn = mm(st, ps[:, hh:hh + 1], PTC[:, hh], ones_col[:], True, True,
                                after=[ex, c1, *freeC[p]])
                    rd = st.put("dve", V.reciprocal, rdC[:], ps[:, 0:H1], after=[dn])
                    go = st.put("dve", V.tensor_tensor, gateO[:], gate[:, H1:2 * H1], along(rdC[:], NE), ALU.mult,
                                after=[rd, gt_])
                    freeC[p] = [rd]
                    st.cut()
            ps, p = pair()
            for h in range(H1):
                o = mm(st, ps[:, h * P:(h + 1) * P], v_sb[:, h], PTC[:, h], True, True, after=[vv, *freeC[p]])
                if h % 4 == 3:
                    i = h // 4
                    chf = ch[:, 4 * i:4 * i + 4].rearrange("p h s -> p (h s)")
                    clf = cl[:, 4 * i:4 * i + 4].rearrange("p h s -> p (h s)")
                    cbf = cb_[:, 4 * i:4 * i + 4].rearrange("p h s -> p (h s)")
                    cx = st.put("act", A.activation, chf, ps[:, 512 * i:512 * i + 512], ACT.Copy, after=[o])
                    st.cut()
                    cz = st.put("pool", G.tensor_copy, cbf, f(chf), after=[cx])
                    cy = st.put("dve", V.tensor_tensor, clf, ps[:, 512 * i:512 * i + 512], f(chf), ALU.subtract,
                                after=[cx])
                    st.cut()
            freeC[p] = [cy]
            for h in range(H1):
                i, de = experts((ch[:, h], cl[:, h], cb_[:, h]), Oh, Ol, h, lambda h, e: gateO[:, h, e:e + 1], go,
                                [cy, cz, cut_done["o", h]])
                dst = accO if h == 0 else FE
                fe = st.put("pool", G.tensor_tensor, dst[:], DE[:, i, 0:2], DE[:, i, 2:4], ALU.add,
                            after=[de, *since("FEread")])
                state["fe", i] = fe
                if h:
                    fe = st.put("pool", G.tensor_tensor, accO[:], accO[:], FE[:], ALU.add, after=[fe])
                    state["FEread"] = fe
                st.cut()
            fe = st.put("pool", G.tensor_tensor, FE[:, 0], accO[:, 0], accO[:, 1], ALU.add, after=[fe])
            rr = st.put("pool", G.tensor_tensor, res[:, k], FE[:, 0], x, ALU.add,
                        after=[fe, *since(("stored", b - 2))])
            state["x3used", b] = state["FEread"] = rr
            state["stored", b] = st.put("sp", SY.dma_start, out[b], res[:, k], sem=s_out[k], by=16, after=[rr])
            return st

        first_loads = loads(0)
        head = Stage(semW)
        head.pieces = [W.pieces[0]]
        W.pieces = W.pieces[1:]
        interleave([head], engines)
        interleave([first_loads], engines)
        for i in range(B + 2):
            now = []
            if i + 1 < B:
                interleave([loads(i + 1)], engines)
            if i < B:
                interleave([load_bias(i)], engines)
            if i == 0:
                now.append(W)
            if i < B:
                now.append(stage_a(i))
            if 0 <= i - 1 < B:
                now.append(stage_b(i - 1))
            if 0 <= i - 2 < B:
                now.append(stage_c(i - 2))
            interleave(now, engines)
        end = [state["stored", b] for b in range(max(0, B - 2), B)]

        totals = {}
        for e in engines.values():
            e.count(totals)

        block = ctx.enter_context(nc.Block())

        @block.tensor
        def _(eng):
            engines["pe"].emit()

        @block.scalar
        def _(eng):
            engines["act"].emit()

        @block.vector
        def _(eng):
            engines["dve"].emit()

        @block.gpsimd
        def _(eng):
            engines["pool"].emit()

        @block.sync
        def _(eng):
            engines["sp"].emit()
            for s in end:
                eng.wait_ge(s.sem, s.count)


_INS = ["x", "ctx_1024", "mask_BxS2_if1", "mask_Bx1xSxS2_ff0", "L0_xattn_Wq", "L0_xattn_bq", "L0_xattn_Wk",
        "L0_xattn_bk", "L0_xattn_Wv", "L0_xattn_bv", "L0_xattn_Wo", "L0_xattn_bo", "L0_ffn_Ws1", "L0_ffn_Ws2",
        "L0_ffn_W1", "L0_ffn_W2", "L0_ffn_Wr", "L1_xattn_wq", "L1_xattn_wk", "L1_xattn_wv", "L1_xattn_wo",
        "L1_ffn_q_w", "L1_ffn_k_w", "L1_ffn_v_w", "L1_ffn_o_w", "L1_ffn_sel_v_w", "L1_ffn_sel_o_w",
        "L1_ffn_route_scale"]


def kernel(**inputs):
    import numpy as np
    import concourse.bacc as bacc
    from concourse.bass_utils import run_bass_kernel_spmd

    nc = bacc.Bacc("TRN2", target_bir_lowering=False, num_devices=1)
    arrays, args = {}, []
    for name in _INS:
        a = np.ascontiguousarray(inputs[name])
        arrays[f"in_{name}"] = a
        args.append(nc.dram_tensor(f"in_{name}", a.shape, mybir.dt.from_np(a.dtype), kind="ExternalInput").ap())
    shape = inputs["x"].shape
    args.append(nc.dram_tensor("out_0", shape, F32, kind="ExternalOutput").ap())
    program(nc, *args)
    r = run_bass_kernel_spmd(nc, [arrays], core_ids=[0])
    return r.results[0]["out_0"]
```

```python
from contextlib import ExitStack

import concourse.bass as bass
from concourse import mybir

F32 = mybir.dt.float32
F32R = mybir.dt.float32r
BF16 = mybir.dt.bfloat16
I32 = mybir.dt.int32
ALU = mybir.AluOpType
ACT = mybir.ActivationFunctionType
AX_X = mybir.AxisListType.X

P = 128
SLOT = 32
RING = 3
MASKED = -1.0e30
EPS = 1e-5
COST = {"act": (55, 0.84), "dve": (68, 1.04), "pool": (120, 3.4), "sp": (650, 0.0), "pe": (110, 0.0)}
SLOWER = {("dve", "reciprocal"): (68, 6.4), ("pool", "tensor_tensor"): (140, 2.0)}
POINTER = 70.0
NOTICE = {"pe": 200.0, "act": 190.0, "dve": 180.0, "pool": 110.0, "sp": 1760.0}
OWN_NOTICE = 60.0
WINDOW = 50.0


class Step:

    def __init__(self, engine, fn, args, kw, after, sem, by, cost):
        self.engine, self.fn, self.args, self.kw = engine, fn, args, kw
        self.after, self.sem, self.by, self.cost = after, sem, by, cost
        self.signals = by > 1
        self.count = 0
        self.then = []
        self.rest = cost
        self.start = None
        self.end = None


class Engine:

    def __init__(self, eng):
        self.eng, self.queue = eng, []

    def count(self, totals):
        for s in self.queue:
            if s.signals:
                totals[s.sem.name] = totals.get(s.sem.name, 0) + s.by
                s.count = totals[s.sem.name]

    def emit(self):
        seen = {}
        for s in self.queue:
            for w in s.after:
                if seen.get(w.sem.name, 0) < w.count:
                    self.eng.wait_ge(w.sem, w.count)
                    seen[w.sem.name] = w.count
            ins = s.fn(*s.args, **s.kw)
            if s.signals:
                ins.then_inc(s.sem, s.by)


class Stage:

    def __init__(self, sems, made):
        self.sems, self.made = sems, made
        self.lines = {}

    def put(self, engine, fn, *args, after=(), sem=None, by=1, cost=None, **kw):
        for w in after:
            w.signals = True
        if cost is None:
            fixed, each = SLOWER.get((engine, fn.__name__), COST[engine])
            sizes = [a.free_size() for a in (*args, *kw.values()) if isinstance(a, bass.AP)]
            cost = fixed + each * (max(sizes) if each else 0) + POINTER * (engine != "pool" and 1 in sizes)
        s = Step(engine, fn, args, kw, list(after), sem or self.sems[engine], by, cost)
        line = self.lines.setdefault(engine, [])
        for w in {*after, *line[-1:]}:
            w.then.append(s)
        line.append(s)
        self.made.append(s)
        return s


def seen(w, s):
    return OWN_NOTICE if w.engine == s.engine else NOTICE[w.engine]


def merge(stages, made, engines):
    for s in reversed(made):
        s.rest += max((t.rest + (seen(s, t) if s in t.after else 0.0) for t in s.then), default=0.0)
    free = {e: 0.0 for e in engines}
    lines = [line[::-1] for st in stages for line in st.lines.values()]
    while lines:
        ready = []
        for line in lines:
            s = line[-1]
            if s.start is None:
                if any(w.end is None for w in s.after):
                    continue
                s.start = max((w.end + seen(w, s) for w in s.after), default=0.0)
            ready.append((max(free[s.engine], s.start), line))
        soon = min(r[0] for r in ready) + WINDOW
        start, line = max((r for r in ready if r[0] <= soon), key=lambda r: r[1][-1].rest)
        s = line.pop()
        s.end = free[s.engine] = start + s.cost
        engines[s.engine].queue.append(s)
        lines = [x for x in lines if x]


def program(nc, x_in, ctx_in, mask_in, bias_in, Wq0, bq0, Wk0, bk0, Wv0, bv0, Wo0, bo0,
            Ws1, Ws2, W1, W2, Wr, wq1, wk1, wv1, wo1, q_w, k_w, v_w, o_w, selv_w, selo_w, rscale,
            out):
    B, S, D = x_in.shape
    assert S == P and D == P
    NH, HD = wq1.shape[1], wq1.shape[2]
    NJ = P // SLOT
    NT = NH // NJ
    E0, F0 = W1.shape[0], W1.shape[2]
    NPAIR = E0 * F0 // P
    NE = 8
    H1 = v_w.shape[0] // NE
    G1 = H1 * NE
    SCALE0 = float(HD) ** -0.5
    SCALE1 = float(P) ** -0.5
    MROW0, ONE_PART = HD, 2
    MROW1 = 3 * HD

    with ExitStack() as ctx:
        def sb(name, shape, dt=F32):
            return ctx.enter_context(nc.sbuf_tensor(name, shape, dt))

        def sem(name):
            return ctx.enter_context(nc.semaphore(name))

        psA = ctx.enter_context(nc.psum_tensor("psA", [P, 2, 512], F32))
        psB = ctx.enter_context(nc.psum_tensor("psB", [P, 2, 512], F32))
        psC = ctx.enter_context(nc.psum_tensor("psC", [P, 2, 1024], F32))

        ident = sb("ident", [P, P])
        ident_r = sb("ident_r", [P, P], F32R)
        ident_b = sb("ident_b", [P, P], BF16)
        causal = sb("causal", [P, P])
        causalT = sb("causalT", [P, P])
        minus_half = sb("minus_half", [P, 1])
        ones_r = sb("ones_r", [P, P], F32R)
        ones32 = sb("ones32", [P, SLOT])
        earlier = sb("earlier", [P, NE])
        WqS0 = sb("WqS0", [P, NH, SLOT], BF16)
        WkS0 = sb("WkS0", [P, NH, SLOT], BF16)
        Wv0b = sb("Wv0b", [P, P], BF16)
        Wo0b = sb("Wo0b", [P, P], BF16)
        bqS = sb("bqS", [P, NT], BF16)
        bkS = sb("bkS", [P, NT], BF16)
        bvb = sb("bvb", [P, P], BF16)
        bob = sb("bob", [P, P], BF16)
        Ws1s = sb("Ws1s", [P, F0])
        Ws2s = sb("Ws2s", [F0, P])
        W1s = sb("W1s", [P, E0, F0])
        W2s = sb("W2s", [P, NPAIR, P])
        Wrs = sb("Wrs", [P, E0])
        WqS1 = sb("WqS1", [P, NH, SLOT])
        WkS1 = sb("WkS1", [P, NH, SLOT])
        Wv1s = sb("Wv1s", [P, P])
        Wo1s = sb("Wo1s", [P, P])
        one_row = sb("one_row", [P, 1])
        less_q = sb("less_q", [P, 1])
        less_k = sb("less_k", [P, 1])
        selT = sb("selT", [P, 2 * G1])
        rs = sb("rs", [P, 1])
        M = sb("M", [P, H1, P])
        Vh = sb("Vh", [P, G1, P], F32R)
        Vl = sb("Vl", [P, G1, P], BF16)
        Oh = sb("Oh", [P, G1, P], F32R)
        Ol = sb("Ol", [P, G1, P], BF16)
        prob_rows = sb("prob_rows", [P, 1])

        x_sb = sb("x_sb", [P, 2, P])
        ctx_sb = sb("ctx_sb", [P, 2, P])
        mrow_i = sb("mrow_i", [P, 2, P], I32)
        mcol_i = sb("mcol_i", [P, 2, 1], I32)
        bias_sb = sb("bias_sb", [P, 2, P])
        ctxT = sb("ctxT", [P, 2, P])
        x2 = sb("x2", [P, 2, P])
        x3 = sb("x3", [P, 2, P])
        res = sb("res", [P, P])

        stA = sb("stA", [P, 6])
        mvA = sb("mvA", [P, 2])
        rsA = sb("rsA", [P, 1])
        xnbA = sb("xnbA", [P, P], BF16)
        xTbA = sb("xTbA", [P, P], BF16)
        ctxTb = sb("ctxTb", [P, P], BF16)
        maskq = sb("maskq", [P, P], BF16)
        maskk = sb("maskk", [P, P], BF16)
        keyrow = sb("keyrow", [P, P])
        keycol = sb("keycol", [P, 1])
        QKb = sb("QKb", [P, 2, NT, P], BF16)
        Qb, Kb = QKb[:, 0], QKb[:, 1]
        UA = QKb.rearrange("p n t s -> p (n t s)").bitcast(F32)
        bdA = sb("bdA", [P, NT, NJ, P], BF16)
        Qs = sb("Qs", [P, NT, P], BF16)
        Ks = sb("Ks", [P, NT, P], BF16)
        Q2 = sb("Q2", [P, NT, P], BF16)
        Vb = sb("Vb", [P, P], BF16)
        Vb2 = sb("Vb2", [P, P], BF16)
        Vaug = sb("Vaug", [P, NH, HD + 1])
        nmA = sb("nmA", [P, NT, NJ])
        MtA = sb("MtA", [P, NT, NJ, SLOT], BF16)
        PTA = sb("PTA", [P, 2, NT, P])
        rdA = sb("rdA", [P, NH])
        atb = sb("atb", [P, NH, HD], BF16)
        atTb = sb("atTb", [P, P], BF16)
        obA = sb("obA", [P, P], BF16)
        ob2 = sb("ob2", [P, P], BF16)
        x1 = sb("x1", [P, P])
        xnA = sb("xnA", [P, P])
        xTA = sb("xTA", [P, P])
        lg = sb("lg", [P, E0])
        top8 = sb("top8", [P, 8])
        gap = sb("gap", [P, 1])
        egap = sb("egap", [P, 1])
        sure = sb("sure", [P, 1])
        prob = sb("prob", [P, E0])
        hg = PTA[:, 0].rearrange("p t s -> p (t s)").rearrange("p (e f) -> p e f", e=E0)
        hT = PTA[:, 1]
        hs = sb("hs", [F0, P])
        hs2 = sb("hs2", [F0, P])

        stB = sb("stB", [P, 6])
        mvB = sb("mvB", [P, 2])
        rsB = sb("rsB", [P, 1])
        xnB = sb("xnB", [P, P])
        xTB = sb("xTB", [P, P])
        bh = sb("bh", [P, P], F32R)
        bl = sb("bl", [P, P], F32R)
        Qh1 = sb("Qh1", [P, NT, P])
        Qs1 = sb("Qs1", [P, NT, P], F32R)
        Ks1 = sb("Ks1", [P, NT, P], F32R)
        Q21 = sb("Q21", [P, NT, P], F32R)
        Vaug1 = sb("Vaug1", [P, NH, HD + 1])
        nmB = sb("nmB", [P, NT, NJ])
        MtB = sb("MtB", [P, NT, NJ, SLOT], F32R)
        PTB = sb("PTB", [P, 2, NT, P])
        rdB = sb("rdB", [P, NH])
        atB = sb("atB", [P, NH, HD])
        atTB = sb("atTB", [P, P])

        stC = sb("stC", [P, 6])
        mvC = sb("mvC", [P, 2])
        rsC = sb("rsC", [P, 1])
        xnC = sb("xnC", [P, P])
        xTC = sb("xTC", [P, P])
        xTh = sb("xTh", [P, P], F32R)
        xTl = sb("xTl", [P, P], F32R)
        xTb = sb("xTb", [P, P], BF16)
        yh = sb("yh", [P, H1, P], F32R)
        yl = sb("yl", [P, H1, P], F32R)
        nmC = sb("nmC", [P, H1])
        lessmax = sb("lessmax", [P, H1, P], F32R)
        den = sb("den", [P, H1 // NJ, P])
        rdC = sb("rdC", [P, H1])
        with nc.sbuf_tensor("PTC", [P, H1, P], F32) as PTC, nc.sbuf_tensor("v_sb", [P, H1, P], F32) as v_sb:
            pass
        ch = sb("ch", [P, H1, P], F32R)
        cl = sb("cl", [P, H1, P], F32R)
        cb_ = sb("cb", [P, H1, P], BF16)
        gp = sb("gp", [P, 2 * H1, NE])
        gt = sb("gt", [P, 2 * H1, NE])
        first = sb("first", [P, 2 * H1, NE])
        second = sb("second", [P, 2 * H1, NE])
        gp2 = sb("gp2", [P, 2 * H1, NE])
        m1 = sb("m1", [P, 2 * H1])
        m2 = sb("m2", [P, 2 * H1])
        r1 = sb("r1", [P, 2 * H1])
        gsum = sb("gsum", [P, 2 * H1])
        gate = sb("gate", [P, 2 * H1, NE])
        gateO = sb("gateO", [P, H1, NE])
        TE = sb("TE", [P, RING, NE // 2, P])
        DE = TE
        accO = sb("accO", [P, NE // 2, P])

        with nc.sbuf_tensor("raw", [P, 2, 1024], F32) as raw:
            pass
        bdB = sb("bdB", [P, NT, NJ, P], F32R)

        def counters(tag):
            return {e: sem(f"{e}_{tag}") for e in ("pe", "act", "dve", "pool", "sp")}

        semW, semA, semB, semC = (counters(t) for t in ("setup", "A", "B", "C"))
        s_in = [sem(f"in{k}") for k in range(2)]
        s_bias = [sem(f"bias{k}") for k in range(2)]
        s_out = [sem(f"out{k}") for k in range(2)]
        s_small = sem("small_weights")
        s_raw = [sem(f"raw{k}") for k in range(2)]

        engines = {"pe": Engine(nc.tensor), "act": Engine(nc.scalar), "dve": Engine(nc.vector),
                   "pool": Engine(nc.gpsimd), "sp": Engine(nc.sync)}
        T, V, A, G, SY = nc.tensor, nc.vector, nc.scalar, nc.gpsimd, nc.sync

        def mm(st, o, l, r, start, stop, after=()):
            n = r.free_size()
            if l.free_size() <= SLOT:
                ns = 69.0
            elif l.dtype == F32:
                ns = max(218.0, 4 * n / 2.4)
            else:
                ns = max(107.0 if l.dtype == F32R else 56.0, n / 2.4)
            return st.put("pe", T.matmul, o, l, r, start=start, stop=stop, after=after, cost=ns)

        def over_heads(ap2, n):
            return ap2.unsqueeze(1).to_broadcast([ap2.shape[0], n, ap2.shape[1]])

        def along(ap2, n):
            return ap2.unsqueeze(2).to_broadcast([ap2.shape[0], ap2.shape[1], n])

        def f(ap):
            return ap.bitcast(F32)

        state = {}

        made = []
        W, IN, SA, SB, SC = (Stage(x, made) for x in (semW, semW, semA, semB, semC))

        def load(dst, src, s, after=()):
            return W.put("sp", SY.dma_start, dst, src, sem=s, by=16, after=after)

        def wide(v, n=P):
            return v.rearrange("(a n) -> a n", a=1).to_broadcast([n, v.shape[0]])

        zi = W.put("pool", G.memset, ident[:], 0.0)
        zi2 = W.put("pool", G.affine_select, out=ident[:], in_=ident[:], compare_op=ALU.not_equal,
                    fill=1.0, base=0, pattern=[[-1, P]], channel_multiplier=1, after=[zi])
        id_r = W.put("pool", G.tensor_copy, ident_r[:], ident[:], after=[zi2])
        id_b = W.put("pool", G.tensor_copy, ident_b[:], ident[:], after=[zi2])
        zc = W.put("pool", G.memset, causal[:], 0.0)
        zct = W.put("pool", G.memset, causalT[:], 0.0)
        cq = W.put("pool", G.affine_select, out=causal[:], in_=causal[:], compare_op=ALU.is_ge,
                   fill=MASKED, base=0, pattern=[[-1, P]], channel_multiplier=1, after=[zc])
        ck = W.put("pool", G.affine_select, out=causalT[:], in_=causalT[:], compare_op=ALU.is_ge,
                   fill=MASKED, base=0, pattern=[[1, P]], channel_multiplier=-1, after=[zct])
        c1 = W.put("pool", G.memset, ones32[:], 1.0)
        ones_done = W.put("act", A.activation, ones_r[:], causal[:], ACT.Identity, bias=1.0, scale=0.0,
                          after=[cq])
        c2 = W.put("pool", G.memset, minus_half[:], -0.5)
        for e in range(NE):
            c3 = W.put("pool", G.memset, earlier[:, e:e + 1], float(NE - e))
        z0 = W.put("pool", G.memset, WqS0[:], 0.0)
        z1 = W.put("pool", G.memset, WkS0[:], 0.0)
        z2 = W.put("pool", G.memset, WqS1[:], 0.0)
        z3 = W.put("pool", G.memset, WkS1[:], 0.0)
        zq = W.put("dve", V.memset, MtA[:], 0.0)
        zr = W.put("dve", V.memset, MtB[:].bitcast(F32), 0.0)
        zbd = W.put("dve", V.memset, bdA[:], 0.0)
        zv = W.put("dve", V.memset, Vaug[:, :, HD:HD + 1], 1.0)
        zv1 = W.put("dve", V.memset, Vaug1[:, :, HD:HD + 1], 1.0)

        rows3 = PTB[0:1, 0].rearrange("p t (j s) -> p t j s", j=NJ)
        w0 = W.put("dve", V.memset, rows3, 0.0)
        wa = W.put("dve", V.memset, rows3[:, 0, :, MROW1:MROW1 + 2], 1.0, after=[w0])
        wb = W.put("dve", V.memset, rows3[:, 1, :, 2 * HD:3 * HD], -1.0, after=[w0])
        wc = W.put("dve", V.memset, rows3[:, 2, :, HD:2 * HD], -1.0, after=[w0])
        wd = W.put("dve", V.memset, rows3[:, 2, :, MROW1:MROW1 + 2], 1.0, after=[w0])
        we = W.put("dve", V.memset, rows3[:, 3, :, MROW0:MROW0 + 2], 1.0, after=[w0])
        bias_rows = PTB[0:NT, 1, 0:2].rearrange("p n (j s) -> p n j s", j=NJ)
        zb = W.put("dve", V.memset, bias_rows, 0.0)
        wq0_raw = raw[:, 0, 0:P]
        wk0_raw = raw[:, 0, P:2 * P]
        wv0_raw = raw[:, 0, 2 * P:3 * P]
        wo0_raw = raw[:, 0, 3 * P:4 * P]
        wq1_raw = raw[:, 0, 4 * P:5 * P]
        wk1_raw = raw[:, 0, 5 * P:6 * P]
        bv_raw = raw[:, 0, 6 * P:7 * P]
        bo_raw = raw[:, 0, 7 * P:8 * P]
        sel_raw = raw[:, 1, 0:P]
        small = []
        for dst, src in ((wq0_raw, Wq0), (wk0_raw, Wk0), (wv0_raw, Wv0), (wo0_raw, Wo0),
                         (wq1_raw, wq1.rearrange("d n h -> d (n h)")),
                         (wk1_raw, wk1.rearrange("d n h -> d (n h)")),
                         (bv_raw, wide(bv0)), (bo_raw, wide(bo0)),
                         (sel_raw[0:G1, :], selv_w), (sel_raw[G1:2 * G1, :], selo_w),
                         (rs[:], wide(rscale)),
                         (Ws1s[:], Ws1), (Ws2s[:], Ws2), (W1s[:], W1.rearrange("e d f -> d e f")),
                         (W2s[:], W2.rearrange("(a e) f d -> (e f) a d", a=NPAIR)),
                         (Wrs[:], Wr),
                         (Wv1s[:], wv1.rearrange("d n h -> d (n h)")),
                         (Wo1s[:], wo1.rearrange("n h d -> (n h) d"))):
            small.append(load(dst, src, s_small))
        for t in range(NT):
            for n, v in enumerate((bq0, bk0)):
                small.append(load(bias_rows[t:t + 1, n, :, 0:HD],
                                  v[t * NJ * HD:(t + 1) * NJ * HD].rearrange("(a j d) -> a j d", a=1, d=HD),
                                  s_small, after=[zb]))
        sm = small[-1]

        sc = W.put("act", A.activation, WqS0[:, :, 0:HD], wq0_raw.rearrange("p (n d) -> p n d", d=HD),
                   ACT.Copy, after=[sm, z0])
        sc = W.put("act", A.activation, WkS0[:, :, 0:HD], wk0_raw.rearrange("p (n d) -> p n d", d=HD),
                   ACT.Copy, after=[z1])
        sc = W.put("act", A.activation, Wv0b[:], wv0_raw, ACT.Copy)
        sc = W.put("act", A.activation, Wo0b[:], wo0_raw, ACT.Copy)
        sc = W.put("act", A.activation, bvb[:], bv_raw, ACT.Copy)
        sc = W.put("act", A.activation, bob[:], bo_raw, ACT.Copy)
        for r in range(3):
            sc = W.put("act", A.mul, WqS1[:, :, r * HD:(r + 1) * HD],
                       wq1_raw.rearrange("p (n d) -> p n d", d=HD), SCALE0, after=[z2])
            sc = W.put("act", A.activation, WkS1[:, :, r * HD:(r + 1) * HD],
                       wk1_raw.rearrange("p (n d) -> p n d", d=HD), ACT.Copy, after=[z3])
        scaled = sc
        for n in range(4):
            tr = mm(W, psA[:, 0, n:n + 1], rows3[:, n].rearrange("a j s -> a (j s)"), ones32[0:1, 0:1],
                    True, True, after=[wa, wb, wc, wd, we, c1])
        tb = mm(W, psA[:, 0, 8:8 + NT], bias_rows[:, 0].rearrange("t j s -> t (j s)"), ident[0:NT, 0:NT],
                True, True, after=[sm, zb, zi2])
        tb = mm(W, psA[:, 0, 16:16 + NT], bias_rows[:, 1].rearrange("t j s -> t (j s)"), ident[0:NT, 0:NT],
                True, True)
        d1 = W.put("dve", V.tensor_copy, one_row[:], psA[:, 0, 0:1], after=[tb])
        d1 = W.put("dve", V.tensor_copy, less_q[:], psA[:, 0, 1:2])
        d1 = W.put("dve", V.tensor_copy, less_k[:], psA[:, 0, 2:3])
        d0 = W.put("dve", V.tensor_copy, prob_rows[:], psA[:, 0, 3:4])
        d1 = W.put("dve", V.tensor_copy, bqS[:], psA[:, 0, 8:8 + NT])
        d1 = W.put("dve", V.tensor_scalar, bkS[:], psA[:, 0, 16:16 + NT], prob_rows[:], None, ALU.add,
                   after=[d0])
        ts = W.put("pe", T.transpose, psA[:, 1, 0:P], sel_raw, ident[:], after=[sm, zi2])
        small_done = W.put("dve", V.tensor_copy, selT[:], psA[:, 1, 0:P], after=[ts])

        qload = load(raw[:, 0, :].rearrange("p (h d) -> p h d", h=H1),
                     q_w.rearrange("(h p) d -> p h d", p=P), s_raw[0], after=[scaled])
        kload = load(raw[:, 1, :].rearrange("p (h d) -> p h d", h=H1),
                     k_w.rearrange("(h p) d -> p h d", p=P), s_raw[1], after=[ts])
        for h in range(H1):
            mh = mm(W, psC[:, 0, h * P:(h + 1) * P], raw[:, 0, h * P:(h + 1) * P],
                    raw[:, 1, h * P:(h + 1) * P], True, True, after=[qload, kload])
        Mdone = W.put("act", A.activation, M[:].rearrange("p h d -> p (h d)"), psC[:, 0, :], ACT.Copy,
                      after=[mh])
        last_read = [Mdone, Mdone]
        cut_done = {}
        n = 0
        for name, src, hi_sb, lo_sb in (("v", v_w, Vh, Vl), ("o", o_w, Oh, Ol)):
            for h in range(H1):
                k = n % 2
                got = load(raw[:, k, :].rearrange("p (e n) -> p e n", e=NE),
                           src[h * NE:(h + 1) * NE].rearrange("e p n -> p e n"), s_raw[k],
                           after=[last_read[k]])
                hsl = hi_sb[:, h * NE:(h + 1) * NE, :].rearrange("p e n -> p (e n)")
                lsl = lo_sb[:, h * NE:(h + 1) * NE, :].rearrange("p e n -> p (e n)")
                hi = W.put("act", A.activation, hsl, raw[:, k, :], ACT.Copy, after=[got])
                lo = W.put("dve", V.tensor_tensor, lsl, raw[:, k, :], f(hsl), ALU.subtract, after=[hi, got])
                last_read[k] = lo
                cut_done[name, h] = lo
                n += 1
        state["bdB_zero"] = W.put("dve", V.memset, bdB[:].bitcast(F32), 0.0, after=last_read)

        def layernorm(st, x, stats, mv, rstd, dst, after):
            a = st.put("dve", V.bn_stats, stats[:], x, after=after)
            a = st.put("dve", V.bn_aggr, mv[:], stats[:], after=[a])
            p = st.put("pool", G.tensor_scalar, rstd[:], mv[:, 1:2], EPS, None, ALU.add, after=[a, c2])
            p = st.put("pool", G.tensor_tensor, rstd[:], rstd[:], minus_half[:], ALU.pow, after=[p])
            return st.put("dve", V.tensor_scalar, dst[:], x, mv[:, 0:1], rstd[:], ALU.subtract, ALU.mult,
                          after=[p])


        def since(*keys):
            return [state[k] for k in keys if k in state]

        def loads(b):
            st = IN
            k = b % 2
            for key, dst, src in (("x1", x_sb[:, k], x_in[b]), ("ctx", ctx_sb[:, k], ctx_in[b]),
                                  ("mask", mrow_i[:, k], wide(mask_in[b])),
                                  ("mask", mcol_i[:, k], mask_in[b].rearrange("(s a) -> s a", a=1))):
                state["in", b] = st.put("sp", SY.dma_start, dst, src, sem=s_in[k], by=16,
                                        after=since((key, b - 2)))

        def load_bias(b):
            st = IN
            state["inbias", b] = st.put("sp", SY.dma_start, bias_sb[:, b % 2], bias_in[b, 0],
                                        sem=s_bias[b % 2], by=16, after=since(("bias", b - 2)))

        def slot_blocks(slots, bd):
            for j in range(NJ):
                rows_j = slice(SLOT * j, SLOT * (j + 1))
                yield bd[rows_j, :, j, :], slots[rows_j]

        def attend(st, ps, free, Qslot, Kslot, Qwithmax, bd, kd, Mt, nm, PT, Vp, U, at, rden,
                   mask_q, mask_k, mrow, scale, ident_mm, ready, vready):
            def scores(t, bank, tiles, pairs, spread_done, after):
                o = ps[:, bank, :].rearrange("p (j s) -> p j s", j=NJ)
                for n, (l, r) in enumerate(pairs):
                    mm(st, o, l, r, n == 0, False, after=after)
                return mm(st, o, tiles[:, t, :], bd[:, t], False, True, after=[spread_done])

            for t in range(NT):
                bank = t % 2
                s = scores(t, bank, Qslot, mask_q, kd, [*ready, *free[bank]])
                m = st.put("dve", V.tensor_reduce, nm[:, t, :], ps[:, bank, :].rearrange("p (j s) -> p j s", j=NJ),
                           AX_X, ALU.max, negate=True, after=[s])
                free[bank] = [m]
            hv = Mt[:, :, :, mrow]
            hi = st.put("dve", V.tensor_copy, hv, nm[:], after=[m])
            lo = st.put("dve", V.tensor_tensor, Mt[:, :, :, mrow + 1], nm[:],
                        f(hv) if Mt.dtype == F32R else hv, ALU.subtract, after=[hi])
            for t in range(NT):
                tp = mm(st, ps[:, 0, t * P:(t + 1) * P], Mt[:, t].rearrange("p j s -> p (j s)"), ident_mm,
                        True, True, after=[lo, *free[0]])
            q = f(Qslot[:]) if Qslot.dtype == F32R else Qslot[:]
            q2 = st.put("dve", V.tensor_tensor, Qwithmax[:], ps[:, 0, :].rearrange("p (t s) -> p t s", t=NT),
                        q, ALU.add, after=[tp])
            free[0] = [q2]
            for to, frm in slot_blocks(Qwithmax, bd):
                qd = st.put("dve", V.tensor_copy, to, frm, after=[q2, s],
                            cost=COST["dve"][0] + 512 * (0.26 if bd.dtype == BF16 else 0.52))
            used = [[], []]
            for t in range(NT):
                s = scores(t, 1, Kslot, mask_k, qd, [*free[1]])
                e = st.put("act", A.activation, PT[:, t % 2].rearrange("p t s -> p (t s)"), ps[:, 1, :],
                           ACT.Exp, scale=scale, after=[s, *used[t % 2]])
                free[1] = [e]
                for j in range(NJ):
                    pv = mm(st, ps[SLOT * j:SLOT * j + HD + 1, 0, t * P:(t + 1) * P], Vp[:, NJ * t + j, :],
                            PT[:, t % 2, j, :], True, True, after=[e, vready, *free[0]])
                used[t % 2] = [pv]
            u = st.put("act", A.activation, U, ps[:, 0, :], ACT.Copy, after=[pv])
            free[0] = [u]
            for t in range(NT):
                tp = st.put("pe", T.transpose, ps[:, 1, t * P:(t + 1) * P], U[:, t * P:(t + 1) * P], ident[:],
                            after=[u, *free[1]])
            o = ps[:, 1, :].rearrange("p (n w) -> p n w", n=NH)
            r = st.put("dve", V.reciprocal, rden[:], o[:, :, HD], after=[tp])
            a = st.put("dve", V.tensor_tensor, at[:], o[:, :, 0:HD], along(rden[:], HD), ALU.mult, after=[r])
            free[1] = [a]
            return a

        freeA = {0: [small_done], 1: [small_done]}
        freeB = {0: [], 1: []}
        freeC = [[[Mdone], [Mdone]], [[Mdone], [Mdone]]]
        s_bdA, s_bdB = sem("bdA"), sem("bdB")

        def stage_a(b):
            st = SA
            k = b % 2
            x = x_sb[:, k]
            loaded = state["in", b]
            mk = st.put("pool", G.tensor_scalar, keyrow[:], mrow_i[:, k], 0, MASKED, ALU.is_le, ALU.mult,
                        after=[loaded, cq, ck, *since(("maskused", b - 1))])
            mk1 = st.put("pool", G.tensor_scalar, keycol[:], mcol_i[:, k], 0, MASKED, ALU.is_le, ALU.mult)
            mk2 = st.put("pool", G.tensor_tensor, maskq[:], keyrow[:], causal[:], ALU.add, after=[mk])
            masks = st.put("pool", G.tensor_scalar, maskk[:], causalT[:], keycol[:], None, ALU.add,
                           after=[mk1])
            state["mask", b] = mk1
            n = layernorm(st, x, stA, mvA, rsA, xnbA, [loaded])
            tc = st.put("pe", T.transpose, psA[:, 1, 0:P], ctx_sb[:, k], ident[:], after=[loaded, zi2, *freeA[1]])
            state["ctx", b] = tc
            cb = st.put("act", A.activation, ctxTb[:], psA[:, 1, 0:P], ACT.Copy, after=[tc])
            cc = st.put("act", A.activation, ctxT[:, k], psA[:, 1, 0:P], ACT.Copy,
                        after=since(("ctxTused", b - 2)))
            state["ctxT", b] = cc
            wq = WqS0[:].rearrange("p n s -> p (n s)")
            wk = WkS0[:].rearrange("p n s -> p (n s)")
            for t in range(NT):
                kk = mm(st, psA[:, 1, t * P:(t + 1) * P], wk[:, t * P:(t + 1) * P], ctxTb[:], True, True,
                        after=[cc, scaled])
            kb = st.put("act", A.activation, Kb.rearrange("p t s -> p (t s)"), psA[:, 1, :], ACT.Copy,
                        after=[kk])
            ks = st.put("pool", G.tensor_tensor, Ks[:], Kb, along(bkS[:], P), ALU.add, after=[kb, small_done])
            for to, frm in slot_blocks(Ks, bdA):
                kd = st.put("sp", SY.dma_start, to, frm, sem=s_bdA, by=16,
                            after=[ks, zbd, *since(("bdA", b - 1))])
            v = mm(st, psA[:, 1, 0:P], ctxTb[:], Wv0b[:], True, True, after=[kb])
            vb = st.put("act", A.activation, Vb[:], psA[:, 1, 0:P], ACT.Copy, after=[v])
            vb2 = st.put("pool", G.tensor_tensor, Vb2[:], Vb[:], bvb[:], ALU.add, after=[vb, scaled])
            va = st.put("act", A.activation, Vaug[:, :, 0:HD], Vb2[:].rearrange("p (n d) -> p n d", d=HD), ACT.Copy,
                        after=[vb2, zv])
            psb = psA[:, 0, 0:64].bitcast(BF16)
            tp = st.put("pe", T.transpose, psb, xnbA[:], ident_b[:], after=[n, id_b, *freeA[0]])
            c = st.put("act", A.activation, xTbA[:], psb, ACT.Copy, after=[tp])
            for t in range(NT):
                q = mm(st, psA[:, 0, t * P:(t + 1) * P], wq[:, t * P:(t + 1) * P], xTbA[:], True, True, after=[c])
            qb = st.put("act", A.activation, Qb.rearrange("p t s -> p (t s)"), psA[:, 0, :], ACT.Copy,
                        after=[q])
            qs = st.put("pool", G.tensor_tensor, Qs[:], Qb, along(bqS[:], P), ALU.add, after=[qb])
            free = {0: [qb], 1: [vb]}
            a = attend(st, psA, free, Qs, Ks, Q2, bdA, kd, MtA, nmA, PTA, Vaug, UA, atb, rdA,
                       [(ident_b[:], over_heads(maskq[:], NT))], [(ident_b[:], over_heads(maskk[:], NT))],
                       MROW0, SCALE0, ident_b[:], [qs, masks, zq], va)
            state["bdA", b] = a
            tp = st.put("pe", T.transpose, psA[:, 1, 0:64].bitcast(BF16), atb[:].rearrange("p n d -> p (n d)"),
                        ident_b[:], after=[a, *free[1]])
            state["maskused", b] = tp
            c = st.put("act", A.activation, atTb[:], psA[:, 1, 0:64].bitcast(BF16), ACT.Copy, after=[tp])
            o = mm(st, psA[:, 0, 0:P], atTb[:], Wo0b[:], True, True, after=[c, *free[0]])
            ob = st.put("act", A.activation, obA[:], psA[:, 0, 0:P], ACT.Copy, after=[o])
            o2 = st.put("pool", G.tensor_tensor, ob2[:], obA[:], bob[:], ALU.add, after=[ob])
            xx = st.put("pool", G.tensor_tensor, x1[:], x, ob2[:], ALU.add, after=[o2])
            state["x1", b] = xx
            n = layernorm(st, x1[:], stA, mvA, rsA, xnA, [xx])
            tp = st.put("pe", T.transpose, psA[:, 1, 0:P], xnA[:], ident[:], after=[n])
            xt = st.put("act", A.activation, xTA[:], psA[:, 1, 0:P], ACT.Copy, after=[tp])
            rl = mm(st, psA[:, 0, 0:E0], xTA[:], Wrs[:], True, True, after=[xt, sm])
            l = st.put("dve", V.tensor_copy, lg[:], psA[:, 0, 0:E0], after=[rl])
            t8 = st.put("dve", V.max, top8[:], lg[:], after=[l])
            gp_ = st.put("dve", V.tensor_tensor, gap[:], top8[:, 1:2], top8[:, 0:1], ALU.subtract, after=[t8])
            hid = mm(st, psA[:, 1, :], xTA[:], W1s[:].rearrange("p e f -> p (e f)"), True, True)
            sh = mm(st, psA[0:F0, 0, 0:P], Ws1s[:], xTA[:], True, True, after=[l])
            eg = st.put("act", A.activation, egap[:], gap[:], ACT.Exp, after=[gp_])
            r_ = st.put("act", A.activation, hs[:], psA[0:F0, 0, 0:P], ACT.Relu, after=[sh])
            r2_ = st.put("act", A.activation, hs2[:], hs[:], ACT.Square, after=[r_])
            su = st.put("dve", V.tensor_scalar, sure[:], egap[:], 1.0, 1.0, ALU.add, ALU.is_equal, after=[eg])
            pr = st.put("dve", V.tensor_scalar, prob[:], lg[:], top8[:, 0:1], sure[:], ALU.is_equal, ALU.mult,
                        after=[su])
            hgs = st.put("dve", V.scalar_tensor_tensor, hg, psA[:, 1, :].rearrange("p (e f) -> p e f", e=E0),
                         0.0, along(prob[:], F0), ALU.max, ALU.mult, after=[pr, hid])
            hgf = hg.rearrange("p e f -> p (e f)")
            for a_ in range(NPAIR):
                tp = st.put("pe", T.transpose, psA[:, 1, a_ * P:(a_ + 1) * P], hgf[:, a_ * P:(a_ + 1) * P],
                            ident[:], after=[hgs])
            hq = st.put("act", A.activation, hT.rearrange("p a s -> p (a s)"), psA[:, 1, :], ACT.Square,
                        after=[tp])
            mm(st, psA[:, 0, 0:P], hs2[:], Ws2s[:], True, False, after=[r2_])
            for a_ in range(NPAIR):
                y = mm(st, psA[:, 0, 0:P], hT[:, a_, :], W2s[:, a_, :], False, a_ == NPAIR - 1, after=[hq])
            xo = st.put("dve", V.tensor_tensor, x2[:, k], psA[:, 0, 0:P], x1[:], ALU.add,
                        after=[y, *since(("x2used", b - 2))])
            state["x2", b] = xo
            freeA[0], freeA[1] = [xo], [hq]

        def stage_b(b):
            st = SB
            k = b % 2
            x = x2[:, k]
            loaded = state["inbias", b]
            b0 = st.put("act", A.activation, bh[:], bias_sb[:, k], ACT.Copy, after=[loaded, *since(("biasused", b - 1))])
            b1 = st.put("pool", G.tensor_tensor, bl[:], bias_sb[:, k], f(bh[:]), ALU.subtract, after=[b0])
            state["bias", b] = b1
            wq = WqS1[:].rearrange("p n s -> p (n s)")
            wk = WkS1[:].rearrange("p n s -> p (n s)")
            Qh1f = Qh1[:].rearrange("p t s -> p (t s)")
            for t in range(NT):
                kk = mm(st, psB[:, 1, t * P:(t + 1) * P], wk[:, t * P:(t + 1) * P], ctxT[:, k], True, True,
                        after=[scaled, state["ctxT", b], *freeB[1]])
            kh = st.put("act", A.activation, Qh1f.bitcast(F32R), psB[:, 1, :], ACT.Identity, bias=one_row[:],
                        after=[kk, small_done])
            k2 = st.put("dve", V.scalar_tensor_tensor, Ks1[:].rearrange("p t s -> p (t s)"), Qh1f, less_k[:],
                        psB[:, 1, :], ALU.mult, ALU.add, after=[kh])
            for to, frm in slot_blocks(Ks1, bdB):
                kd = st.put("sp", SY.dma_start, f(to), f(frm), sem=s_bdB, by=16,
                            after=[k2, state["bdB_zero"], *since(("bdB", b - 1))])
            v = mm(st, psB[:, 1, 0:P], ctxT[:, k], Wv1s[:], True, True, after=[k2, sm])
            state["ctxTused", b] = v
            va = st.put("act", A.activation, Vaug1[:, :, 0:HD],
                        psB[:, 1, 0:P].rearrange("p (n d) -> p n d", d=HD), ACT.Copy, after=[v, zv1])
            n = layernorm(st, x, stB, mvB, rsB, xnB, [state["x2", b]])
            tp = st.put("pe", T.transpose, psB[:, 0, 0:P], xnB[:], ident[:], after=[n, zi2, *freeB[0]])
            c = st.put("act", A.activation, xTB[:], psB[:, 0, 0:P], ACT.Copy, after=[tp])
            for t in range(NT):
                q = mm(st, psB[:, 0, t * P:(t + 1) * P], wq[:, t * P:(t + 1) * P], xTB[:], True, True, after=[c])
            qh = st.put("act", A.activation, Qh1f.bitcast(F32R), psB[:, 0, :], ACT.Copy, after=[q, k2])
            q2 = st.put("dve", V.scalar_tensor_tensor, Qs1[:].rearrange("p t s -> p (t s)"), Qh1f, less_q[:],
                        psB[:, 0, :], ALU.mult, ALU.add, after=[qh])
            free = {0: [q2], 1: [va]}
            a = attend(st, psB, free, Qs1, Ks1, Q21, bdB, kd, MtB, nmB, PTB, Vaug1, Qh1f, atB, rdB,
                       [(ident_r[:], over_heads(bh[:], NT)), (ident_r[:], over_heads(bl[:], NT))],
                       [(bh[:], over_heads(ident_r[:], NT)), (bl[:], over_heads(ident_r[:], NT))],
                       MROW1, 1.0, ident_r[:], [q2, b1, id_r, zr], va)
            state["bdB", b] = a
            tp = st.put("pe", T.transpose, psB[:, 1, 0:P], atB[:].rearrange("p n d -> p (n d)"), ident[:],
                        after=[a, *free[1]])
            state["biasused", b] = tp
            c = st.put("act", A.activation, atTB[:], psB[:, 1, 0:P], ACT.Copy, after=[tp])
            o = mm(st, psB[:, 0, 0:P], atTB[:], Wo1s[:], True, True, after=[c, *free[0]])
            xo = st.put("dve", V.tensor_tensor, x3[:, k], psB[:, 0, 0:P], x, ALU.add,
                        after=[o, *since(("x3used", b - 2))])
            state["x2used", b] = xo
            state["x3", b] = xo
            freeB[0], freeB[1] = [xo], [c]

        turn = [0]

        parity = [0]

        def pair():
            p = turn[0] % 2
            turn[0] += 1
            return psC[:, p], p

        def experts(lhs, w_hi, w_lo, h, g_of, gates_ready, after):
            st = SC
            i = parity[0] % RING
            parity[0] += 1
            ps, p = pair()
            for half in (1, 0):
                o = ps[:, 512 * half:512 * half + 512]
                e0 = h * NE + half * (NE // 2)
                wh = w_hi[:, e0:e0 + NE // 2].rearrange("p e n -> p (e n)")
                wl = w_lo[:, e0:e0 + NE // 2].rearrange("p e n -> p (e n)")
                mm(st, o, lhs[0], wh, True, False, after=[*after, *freeC[p][half]])
                mm(st, o, lhs[1], wh, False, False)
                z = mm(st, o, lhs[2], wl, False, True)
                if half:
                    z1_ = z
            te = []
            for e in range(NE // 2):
                te.append(st.put("act", A.activation, TE[:, i, e], ps[:, 512 + e * P:512 + (e + 1) * P],
                                 ACT.Copy, scale=g_of(h, e + NE // 2),
                                 after=[z1_, gates_ready, *since(("fe", i))]))
            for e in range(NE // 2):
                de = st.put("dve", V.scalar_tensor_tensor, DE[:, i, e], ps[:, e * P:(e + 1) * P],
                            g_of(h, e), TE[:, i, e], ALU.mult, ALU.add,
                            after=[z, te[e], gates_ready, *since(("fe", i))])
            freeC[p][:] = [de], [te[-1]]
            state["de", i] = de
            return i, de

        def head(b):
            st = SC
            k = b % 2
            x = x3[:, k]
            n = layernorm(st, x, stC, mvC, rsC, xnC, [state["x3", b]])
            yield
            ps, p = pair()
            tp = st.put("pe", T.transpose, ps[:, 0:P], xnC[:], ident[:], after=[n, zi2, *freeC[p][0]])
            h_ = st.put("act", A.activation, xTh[:], ps[:, 0:P], ACT.Copy, after=[tp])
            c = st.put("act", A.activation, xTC[:], ps[:, 0:P], ACT.Copy)
            xb_ = st.put("act", A.activation, xTb[:], ps[:, 0:P], ACT.Copy)
            l_ = st.put("dve", V.tensor_tensor, xTl[:], ps[:, 0:P], f(xTh[:]), ALU.subtract, after=[h_, xb_])
            gl = mm(st, ps[:, 512:512 + 2 * G1], xTC[:], selT[:], True, True,
                    after=[c, small_done, *freeC[p][1]])
            gpf = gp[:].rearrange("p g e -> p (g e)")
            e_ = st.put("act", A.activation, gpf, ps[:, 512:512 + 2 * G1], ACT.Exp, scale=-1.0, after=[gl])
            freeC[p][:] = [l_], [e_]
            g = st.put("dve", V.tensor_scalar, gpf, gpf, 1.0, None, ALU.add, after=[e_])
            yield
            ps, p = pair()
            for h in range(H1):
                y = mm(st, ps[:, h * P:(h + 1) * P], M[:, h], xTC[:], True, True, after=[c, Mdone, *freeC[p][h // 4]])
                if h % 4 == 3:
                    i = h // 4
                    yhf = yh[:, 4 * i:4 * i + 4].rearrange("p h s -> p (h s)")
                    ylf = yl[:, 4 * i:4 * i + 4].rearrange("p h s -> p (h s)")
                    yy = st.put("act", A.activation, yhf, ps[:, 512 * i:512 * i + 512], ACT.Copy, after=[y])
                    yx = st.put("dve", V.tensor_tensor, ylf, ps[:, 512 * i:512 * i + 512], f(yhf), ALU.subtract,
                                after=[yy])
                    freeC[p][i] = [yx]
            g = st.put("dve", V.reciprocal, gpf, gpf, after=[g])
            g = st.put("dve", V.tensor_reduce, m1[:], gp[:], AX_X, ALU.max, after=[g])

            def first_best(src, best, dst, after):
                a = st.put("dve", V.tensor_tensor, gt[:], src[:], along(best[:], NE), ALU.is_equal, after=after)
                a = st.put("dve", V.tensor_tensor, gt[:], gt[:], over_heads(earlier[:], 2 * H1), ALU.mult,
                           after=[a, c3])
                a = st.put("dve", V.tensor_reduce, r1[:], gt[:], AX_X, ALU.max, after=[a])
                return st.put("dve", V.tensor_tensor, dst[:], gt[:], along(r1[:], NE), ALU.is_equal, after=[a])

            g = first_best(gp, m1, first, [g])
            yield
            ps, p = pair()
            for h in range(H1):
                s = mm(st, ps[:, h * P:(h + 1) * P], yh[:, h], xTh[:], True, True, after=[yy, *freeC[p][h // 4]])
            g = st.put("dve", V.scalar_tensor_tensor, gp2[:].rearrange("p g e -> p (g e)"),
                       first[:].rearrange("p g e -> p (g e)"), -2.0, gpf, ALU.mult, ALU.add, after=[g])
            g = st.put("dve", V.tensor_reduce, m2[:], gp2[:], AX_X, ALU.max, after=[g])
            g = first_best(gp2, m2, second, [g])
            dg = []
            for i in range(H1 // 4):
                four = slice(4 * i, 4 * i + 4)
                nm = st.put("dve", V.tensor_reduce, nmC[:, four],
                            ps[:, 512 * i:512 * i + 512].rearrange("p (h s) -> p h s", h=4), AX_X,
                            ALU.max, negate=True, after=[s])
                dg.append(st.put("pool", G.tensor_tensor, lessmax[:, four], over_heads(ident[:], 4),
                                 along(nmC[:, four], P), ALU.mult, after=[nm, *since(("lessmax", b - 1))]))
                freeC[p][i] = [nm]
            q = st.put("dve", V.tensor_tensor, gsum[:], m1[:], m2[:], ALU.add, after=[g])
            q = st.put("dve", V.tensor_scalar, gsum[:], gsum[:], 1e-9, None, ALU.max, after=[q])
            q = st.put("dve", V.reciprocal, gsum[:], gsum[:], after=[q])
            q = st.put("dve", V.tensor_scalar, gsum[:], gsum[:], rs[:], None, ALU.mult, after=[q, sm])
            q1 = st.put("dve", V.tensor_tensor, m1[:], m1[:], gsum[:], ALU.mult, after=[q])
            q2 = st.put("dve", V.tensor_tensor, m2[:], m2[:], gsum[:], ALU.mult, after=[q])
            q1 = st.put("pool", G.tensor_tensor, first[:], first[:], along(m1[:], NE), ALU.mult, after=[q2])
            q2 = st.put("pool", G.tensor_tensor, second[:], second[:], along(m2[:], NE), ALU.mult)
            gt_ = st.put("pool", G.tensor_tensor, gate[:], first[:], second[:], ALU.add, after=[q1, q2])
            yield
            ps, p = pair()
            for i in range(H1 // 4):
                o = ps[:, 512 * i:512 * i + 512]
                yhf = yh[:, 4 * i:4 * i + 4].rearrange("p h s -> p (h s)")
                ylf = yl[:, 4 * i:4 * i + 4].rearrange("p h s -> p (h s)")
                mm(st, o, xTh[:], yhf, True, False, after=[*freeC[p][i]])
                mm(st, o, xTh[:], ylf, False, False, after=[yx])
                mm(st, o, xTl[:], yhf, False, False)
                s = mm(st, o, ones_r[:], lessmax[:, 4 * i:4 * i + 4].rearrange("p h s -> p (h s)"), False, True,
                       after=[dg[i], ones_done])
                ex = st.put("act", A.activation, PTC[:, 4 * i:4 * i + 4].rearrange("p h s -> p (h s)"), o,
                            ACT.Exp, scale=SCALE1, after=[s])
                freeC[p][i] = [ex]
            state["lessmax", b] = ex

            state["C", b] = ex, xb_, gt_

        def values(b):
            st = SC
            ex, xb_, gt_ = state["C", b]
            summed = []
            for h in range(H1):
                i, de = experts((xTh[:], xTl[:], xTb[:]), Vh, Vl, h, lambda h, e: gate[:, h, e:e + 1], gt_,
                                [cut_done["v", h], xb_])
                fe = st.put("pool", G.tensor_tensor, DE[:, i, 0:2], DE[:, i, 0:2], DE[:, i, 2:4], ALU.add, after=[de])
                vv = st.put("pool", G.tensor_tensor, v_sb[:, h], DE[:, i, 0], DE[:, i, 1], ALU.add, after=[fe])
                state["fe", i] = vv
                summed.append(vv)
                yield
                if h == 2:
                    ps, p = pair()
                    for hh in range(H1):
                        j, t = hh % NJ, hh // NJ
                        dn = mm(st, ps[SLOT * j:SLOT * (j + 1), t * P:(t + 1) * P], ones32[:], PTC[:, hh], True, True,
                                after=[ex, c1, *freeC[p][0]])
                    dc = st.put("act", A.activation, den[:].rearrange("p t s -> p (t s)"), ps[:, 0:H1 // NJ * P],
                                ACT.Copy, after=[dn])
                    for t in range(H1 // NJ):
                        dn = st.put("pe", T.transpose, ps[:, 512 + t * P:512 + (t + 1) * P], den[:, t], ident[:],
                                    after=[dc, *freeC[p][1]])
                    rd = st.put("dve", V.reciprocal, rdC[:],
                                ps[:, 512:512 + H1 * SLOT].rearrange("p (h s) -> p h s", s=SLOT)[:, :, 0],
                                after=[dn])
                    go = st.put("dve", V.tensor_tensor, gateO[:], gate[:, H1:2 * H1], along(rdC[:], NE), ALU.mult,
                                after=[rd, gt_])
                    freeC[p][:] = [dc], [rd]
            cut = []
            ps, p = pair()
            for h in range(H1):
                o = mm(st, ps[:, h * P:(h + 1) * P], v_sb[:, h], PTC[:, h], True, True, after=[summed[h], *freeC[p][h // 4]])
                if h % 4 == 3:
                    i = h // 4
                    chf = ch[:, 4 * i:4 * i + 4].rearrange("p h s -> p (h s)")
                    clf = cl[:, 4 * i:4 * i + 4].rearrange("p h s -> p (h s)")
                    cbf = cb_[:, 4 * i:4 * i + 4].rearrange("p h s -> p (h s)")
                    cx = st.put("act", A.activation, chf, ps[:, 512 * i:512 * i + 512], ACT.Copy, after=[o])
                    cz = st.put("act", A.activation, cbf, f(chf), ACT.Copy, after=[cx])
                    cy = st.put("dve", V.tensor_tensor, clf, ps[:, 512 * i:512 * i + 512], f(chf), ALU.subtract,
                                after=[cx])
                    freeC[p][i] = [cy]
                    cut.append([cy, cz])
            state["context", b] = go, cut

        def output(b):
            st = SC
            k = b % 2
            x = x3[:, k]
            go, cut = state["context", b]
            for h in range(H1):
                i, de = experts((ch[:, h], cl[:, h], cb_[:, h]), Oh, Ol, h, lambda h, e: gateO[:, h, e:e + 1], go,
                                [*cut[h // 4], cut_done["o", h]])
                if h:
                    before = accO[:] if h > 1 else DE[:, first_i]
                    fe = st.put("pool", G.tensor_tensor, accO[:], before, DE[:, i], ALU.add,
                                after=[de, *([fe] if h > 1 else since("accOread"))])
                    state["fe", i] = fe
                    if h == 1:
                        state["fe", first_i] = fe
                else:
                    first_i = i
                yield
            fe = st.put("pool", G.tensor_tensor, accO[:, 0:2], accO[:, 0:2], accO[:, 2:4], ALU.add, after=[fe])
            fe = st.put("pool", G.tensor_tensor, accO[:, 0], accO[:, 0], accO[:, 1], ALU.add, after=[fe])
            rr = st.put("pool", G.tensor_tensor, res[:], accO[:, 0], x, ALU.add,
                        after=[fe, *since(("stored", b - 1))])
            state["x3used", b] = state["accOread"] = rr
            state["stored", b] = st.put("sp", SY.dma_start, out[b], res[:], sem=s_out[k], by=16, after=[rr])

        def run(parts, count=None):
            n = 0
            while n != count and next(parts, parts) is not parts:
                n += 1

        def stage_c(b):
            if b == 0:
                nxt = head(0)
                run(nxt)
            body = values(b)
            nxt = head(b + 1) if b + 1 < B else iter(())
            run(body, 6)
            run(nxt, 1)
            run(body)
            tail = output(b)
            for some in (2, 2, 2):
                run(tail, some)
                run(nxt, 1)
            run(tail)
            run(nxt)

        loads(0)
        for i in range(B + 2):
            if i + 1 < B:
                loads(i + 1)
            if i < B:
                load_bias(i)
                stage_a(i)
            if 0 <= i - 1 < B:
                stage_b(i - 1)
            if 0 <= i - 2 < B:
                stage_c(i - 2)
        merge([IN, SC, SA, SB, W], made, engines)
        end = [state["stored", b] for b in range(max(0, B - 2), B)]

        totals = {}
        for e in engines.values():
            e.count(totals)

        block = ctx.enter_context(nc.Block())

        @block.tensor
        def _(eng):
            engines["pe"].emit()

        @block.scalar
        def _(eng):
            engines["act"].emit()

        @block.vector
        def _(eng):
            engines["dve"].emit()

        @block.gpsimd
        def _(eng):
            engines["pool"].emit()

        @block.sync
        def _(eng):
            engines["sp"].emit()
            for s in end:
                eng.wait_ge(s.sem, s.count)


_INS = ["x", "ctx_1024", "mask_BxS2_if1", "mask_Bx1xSxS2_ff0", "L0_xattn_Wq", "L0_xattn_bq", "L0_xattn_Wk",
        "L0_xattn_bk", "L0_xattn_Wv", "L0_xattn_bv", "L0_xattn_Wo", "L0_xattn_bo", "L0_ffn_Ws1", "L0_ffn_Ws2",
        "L0_ffn_W1", "L0_ffn_W2", "L0_ffn_Wr", "L1_xattn_wq", "L1_xattn_wk", "L1_xattn_wv", "L1_xattn_wo",
        "L1_ffn_q_w", "L1_ffn_k_w", "L1_ffn_v_w", "L1_ffn_o_w", "L1_ffn_sel_v_w", "L1_ffn_sel_o_w",
        "L1_ffn_route_scale"]


def kernel(**inputs):
    import numpy as np
    import concourse.bacc as bacc
    from concourse.bass_utils import run_bass_kernel_spmd

    nc = bacc.Bacc("TRN2", target_bir_lowering=False, num_devices=1)
    arrays, args = {}, []
    for name in _INS:
        a = np.ascontiguousarray(inputs[name])
        arrays[f"in_{name}"] = a
        args.append(nc.dram_tensor(f"in_{name}", a.shape, mybir.dt.from_np(a.dtype), kind="ExternalInput").ap())
    shape = inputs["x"].shape
    args.append(nc.dram_tensor("out_0", shape, F32, kind="ExternalOutput").ap())
    program(nc, *args)
    r = run_bass_kernel_spmd(nc, [arrays], core_ids=[0])
    return r.results[0]["out_0"]
```

```python
from contextlib import ExitStack

import concourse.bass as bass
from concourse import mybir

F32 = mybir.dt.float32
F32R = mybir.dt.float32r
BF16 = mybir.dt.bfloat16
I32 = mybir.dt.int32
ALU = mybir.AluOpType
ACT = mybir.ActivationFunctionType
AX_X = mybir.AxisListType.X

P = 128
SLOT = 32
RING = 3
TAKEN = -3.0e38
MASKED = -1.0e30
EPS = 1e-5
COST = {"act": (55, 0.84), "dve": (68, 1.04), "pool": (120, 3.4), "sp": (600, 0.0), "pe": (110, 0.0)}
SLOWER = {("dve", "reciprocal"): (68, 6.4), ("pool", "tensor_tensor"): (140, 2.0),
          ("pool", "affine_select"): (127, 0.91)}
POINTER = 70.0
NOTICE = {"pe": 200.0, "act": 220.0, "dve": 180.0, "pool": 110.0, "sp": 1760.0}
OWN_NOTICE = 60.0
WINDOW = 50.0


class Step:

    def __init__(self, engine, fn, args, kw, after, sem, by, cost):
        self.engine, self.fn, self.args, self.kw = engine, fn, args, kw
        self.after, self.sem, self.by, self.cost = after, sem, by, cost
        self.signals = by > 1
        self.count = 0
        self.then = []
        self.rest = cost
        self.start = None
        self.end = None


class Engine:

    def __init__(self, eng):
        self.eng, self.queue = eng, []

    def count(self, totals):
        for s in self.queue:
            if s.signals:
                totals[s.sem.name] = totals.get(s.sem.name, 0) + s.by
                s.count = totals[s.sem.name]

    def emit(self):
        reached = {}
        for s in self.queue:
            waits = {}
            for w in s.after:
                if reached.get(w.sem.name, 0) < w.count:
                    reached[w.sem.name] = w.count
                    waits[w.sem.name] = w
            for w in sorted(waits.values(), key=lambda w: -w.end - seen(w, s)):
                self.eng.wait_ge(w.sem, w.count)
            ins = s.fn(*s.args, **s.kw)
            if s.signals:
                ins.then_inc(s.sem, s.by)


class Stage:

    def __init__(self, sems, made):
        self.sems, self.made = sems, made
        self.lines = {}

    def put(self, engine, fn, *args, after=(), sem=None, by=1, cost=None, **kw):
        for w in after:
            w.signals = True
        if cost is None:
            fixed, each = SLOWER.get((engine, fn.__name__), COST[engine])
            sizes = [a.free_size() for a in (*args, *kw.values()) if isinstance(a, bass.AP)]
            cost = fixed + each * (max(sizes) if each else 0) + POINTER * (engine != "pool" and 1 in sizes)
        s = Step(engine, fn, args, kw, list(after), sem or self.sems[engine], by, cost)
        line = self.lines.setdefault(engine, [])
        for w in {*after, *line[-1:]}:
            w.then.append(s)
        line.append(s)
        self.made.append(s)
        return s


def seen(w, s):
    return OWN_NOTICE if w.engine == s.engine else NOTICE[w.engine]


def merge(stages, made, engines):
    for s in reversed(made):
        s.rest += max((t.rest + (seen(s, t) if s in t.after else 0.0) for t in s.then), default=0.0)
    free = {e: 0.0 for e in engines}
    lines = [line[::-1] for st in stages for line in st.lines.values()]
    while lines:
        ready = []
        for line in lines:
            s = line[-1]
            if s.start is None:
                if any(w.end is None for w in s.after):
                    continue
                s.start = max((w.end + seen(w, s) for w in s.after), default=0.0)
            ready.append((max(free[s.engine], s.start), line))
        soon = min(r[0] for r in ready) + WINDOW
        start, line = max((r for r in ready if r[0] <= soon), key=lambda r: r[1][-1].rest)
        s = line.pop()
        s.end = free[s.engine] = start + s.cost
        engines[s.engine].queue.append(s)
        lines = [x for x in lines if x]


def program(nc, x_in, ctx_in, mask_in, bias_in, Wq0, bq0, Wk0, bk0, Wv0, bv0, Wo0, bo0,
            Ws1, Ws2, W1, W2, Wr, wq1, wk1, wv1, wo1, q_w, k_w, v_w, o_w, selv_w, selo_w, rscale,
            out):
    B, S, D = x_in.shape
    assert S == P and D == P
    NH, HD = wq1.shape[1], wq1.shape[2]
    NJ = P // SLOT
    NT = NH // NJ
    E0, F0 = W1.shape[0], W1.shape[2]
    NPAIR = E0 * F0 // P
    NE = 8
    H1 = v_w.shape[0] // NE
    G1 = H1 * NE
    SCALE0 = float(HD) ** -0.5
    SCALE1 = float(P) ** -0.5
    MROW0 = HD
    MROW1 = 3 * HD

    with ExitStack() as ctx:
        def sb(name, shape, dt=F32):
            return ctx.enter_context(nc.sbuf_tensor(name, shape, dt))

        def sem(name):
            return ctx.enter_context(nc.semaphore(name))

        psA = ctx.enter_context(nc.psum_tensor("psA", [P, 2, 512], F32))
        psB = ctx.enter_context(nc.psum_tensor("psB", [P, 2, 512], F32))
        psC = ctx.enter_context(nc.psum_tensor("psC", [P, 2, 1024], F32))

        ident = sb("ident", [P, P])
        ident_r = sb("ident_r", [P, P], F32R)
        ident_b = sb("ident_b", [P, P], BF16)
        causal = sb("causal", [P, P])
        minus_half = sb("minus_half", [P, 1])
        ones_r = sb("ones_r", [P, P], F32R)
        ones32 = sb("ones32", [P, SLOT])
        earlier = sb("earlier", [P, NE])
        WqS0 = sb("WqS0", [P, NH, SLOT], BF16)
        WkS0 = sb("WkS0", [P, NH, SLOT], BF16)
        Wv0b = sb("Wv0b", [P, P], BF16)
        Wo0b = sb("Wo0b", [P, P], BF16)
        bqS = sb("bqS", [P, NT], BF16)
        bkS = sb("bkS", [P, NT], BF16)
        bvb = sb("bvb", [P, P], BF16)
        bob = sb("bob", [P, P], BF16)
        Ws1s = sb("Ws1s", [P, F0])
        Ws2s = sb("Ws2s", [F0, P])
        W1s = sb("W1s", [P, E0, F0])
        W2s = sb("W2s", [P, NPAIR, P])
        Wrs = sb("Wrs", [P, E0])
        WqS1 = sb("WqS1", [P, NH, SLOT])
        WkS1 = sb("WkS1", [P, NH, SLOT])
        Wv1s = sb("Wv1s", [P, P])
        Wo1s = sb("Wo1s", [P, P])
        one_row = sb("one_row", [P, 1])
        less_q = sb("less_q", [P, 1])
        less_k = sb("less_k", [P, 1])
        selT = sb("selT", [P, 2 * G1])
        rs = sb("rs", [P, 1])
        M = sb("M", [P, H1, P])
        Vh = sb("Vh", [P, G1, P], F32R)
        Vl = sb("Vl", [P, G1, P], BF16)
        Oh = sb("Oh", [P, G1, P], F32R)
        Ol = sb("Ol", [P, G1, P], BF16)
        max_rows = sb("max_rows", [P, 1])

        x_sb = sb("x_sb", [P, 2, P])
        ctx_sb = sb("ctx_sb", [P, 2, P])
        mrow_i = sb("mrow_i", [P, 2, P], I32)
        mcol_i = sb("mcol_i", [P, 2, 1], I32)
        bias_sb = sb("bias_sb", [P, 2, P])
        ctxT = sb("ctxT", [P, 2, P])
        x2 = sb("x2", [P, 2, P])
        x3 = sb("x3", [P, 2, P])
        res = sb("res", [P, P])

        stA = sb("stA", [P, 6])
        mvA = sb("mvA", [P, 2])
        rsA = sb("rsA", [P, 1])
        xnbA = sb("xnbA", [P, P], BF16)
        xTbA = sb("xTbA", [P, P], BF16)
        ctxTb = sb("ctxTb", [P, P], BF16)
        maskq = sb("maskq", [P, P], BF16)
        keyrow = sb("keyrow", [P, P])
        keycol = sb("keycol", [P, 1])
        QKb = sb("QKb", [P, 2, NT, P], BF16)
        Qb, Kb = QKb[:, 0], QKb[:, 1]
        UA = QKb.rearrange("p n t s -> p (n t s)").bitcast(F32)
        bdA = sb("bdA", [P, NT, NJ, P], BF16)
        Qs = sb("Qs", [P, NT, P], BF16)
        Ks = sb("Ks", [P, NT, P], BF16)
        Q2 = sb("Q2", [P, NT, P], BF16)
        Vb = sb("Vb", [P, P], BF16)
        Vb2 = sb("Vb2", [P, P], BF16)
        Vaug = sb("Vaug", [P, NH, HD + 1])
        nmA = sb("nmA", [P, NT, NJ])
        MtA = sb("MtA", [P, NT, NJ, SLOT], BF16)
        PTA = sb("PTA", [P, 2, NT, P])
        rdA = sb("rdA", [P, NH])
        atb = sb("atb", [P, NH, HD], BF16)
        atTb = sb("atTb", [P, P], BF16)
        obA = sb("obA", [P, P], BF16)
        ob2 = sb("ob2", [P, P], BF16)
        x1 = sb("x1", [P, P])
        xnA = sb("xnA", [P, P])
        xTA = sb("xTA", [P, P])
        lg = sb("lg", [P, E0])
        top8 = sb("top8", [P, 8])
        gap = sb("gap", [P, 1])
        egap = sb("egap", [P, 1])
        sure = sb("sure", [P, 1])
        prob = sb("prob", [P, E0])
        hg = PTA[:, 0].rearrange("p t s -> p (t s)").rearrange("p (e f) -> p e f", e=E0)
        hT = PTA[:, 1]
        hs = sb("hs", [F0, P])
        hs2 = sb("hs2", [F0, P])

        stB = sb("stB", [P, 6])
        mvB = sb("mvB", [P, 2])
        rsB = sb("rsB", [P, 1])
        xnB = sb("xnB", [P, P])
        xTB = sb("xTB", [P, P])
        bh = sb("bh", [P, P], F32R)
        bl = sb("bl", [P, P], F32R)
        Qh1 = sb("Qh1", [P, NT, P])
        Qs1 = sb("Qs1", [P, NT, P], F32R)
        Ks1 = sb("Ks1", [P, NT, P], F32R)
        Q21 = sb("Q21", [P, NT, P], F32R)
        Vaug1 = sb("Vaug1", [P, NH, HD + 1])
        nmB = sb("nmB", [P, NT, NJ])
        MtB = sb("MtB", [P, NT, NJ, SLOT], F32R)
        PTB = sb("PTB", [P, 2, NT, P])
        rdB = sb("rdB", [P, NH])
        atB = sb("atB", [P, NH, HD])
        atTB = sb("atTB", [P, P])

        stC = sb("stC", [P, 6])
        mvC = sb("mvC", [P, 2])
        rsC = sb("rsC", [P, 1])
        xnC = sb("xnC", [P, P])
        xTC = sb("xTC", [P, P])
        xTh = sb("xTh", [P, P], F32R)
        xTl = sb("xTl", [P, P], F32R)
        xTb = sb("xTb", [P, P], BF16)
        yh = sb("yh", [P, H1, P], F32R)
        yl = sb("yl", [P, H1, P], F32R)
        nmC = sb("nmC", [P, H1])
        lessmax = sb("lessmax", [P, H1, P], F32R)
        den = sb("den", [P, H1 // NJ, P])
        rdC = sb("rdC", [P, H1])
        with nc.sbuf_tensor("PTC", [P, H1, P], F32) as PTC, nc.sbuf_tensor("v_sb", [P, H1, P], F32) as v_sb:
            pass
        ch = sb("ch", [P, H1, P], F32R)
        cl = sb("cl", [P, H1, P], F32R)
        cb_ = sb("cb", [P, H1, P], BF16)
        gp = sb("gp", [P, 2 * H1, NE])
        gt = sb("gt", [P, 2 * H1, NE])
        first = sb("first", [P, 2 * H1, NE])
        second = sb("second", [P, 2 * H1, NE])
        gp2 = sb("gp2", [P, 2 * H1, NE])
        best2 = sb("best2", [P, 2, 2 * H1])
        m1, m2 = best2[:, 0], best2[:, 1]
        r1 = sb("r1", [P, 2 * H1])
        gsum = sb("gsum", [P, 2 * H1])
        gate = sb("gate", [P, 2 * H1, NE])
        gateO = sb("gateO", [P, H1, NE])
        TE = sb("TE", [P, RING, NE // 2, P])
        DE = TE
        accO = sb("accO", [P, NE // 2, P])

        with nc.sbuf_tensor("raw", [P, 2, 1024], F32) as raw:
            pass
        bdB = sb("bdB", [P, NT, NJ, P], F32R)

        def counters(tag):
            return {e: sem(f"{e}_{tag}") for e in ("pe", "act", "dve", "pool", "sp")}

        semW, semA, semB, semC = (counters(t) for t in ("setup", "A", "B", "C"))
        s_in = [sem(f"in{k}") for k in range(2)]
        s_bias = [sem(f"bias{k}") for k in range(2)]
        s_out = [sem(f"out{k}") for k in range(2)]
        s_weights = [sem(f"weights{k}") for k in range(5)]
        s_raw = [sem(f"raw{k}") for k in range(2)]

        engines = {"pe": Engine(nc.tensor), "act": Engine(nc.scalar), "dve": Engine(nc.vector),
                   "pool": Engine(nc.gpsimd), "sp": Engine(nc.sync)}
        T, V, A, G, SY = nc.tensor, nc.vector, nc.scalar, nc.gpsimd, nc.sync

        def mm(st, o, l, r, start, stop, after=()):
            n = r.free_size()
            if l.free_size() <= SLOT:
                ns = 69.0
            elif l.dtype == F32:
                ns = max(218.0, 4 * n / 2.4)
            else:
                ns = max(107.0 if l.dtype == F32R else 56.0, n / 2.4)
            return st.put("pe", T.matmul, o, l, r, start=start, stop=stop, after=after, cost=ns)

        def over_heads(ap2, n):
            return ap2.unsqueeze(1).to_broadcast([ap2.shape[0], n, ap2.shape[1]])

        def along(ap2, n):
            return ap2.unsqueeze(2).to_broadcast([ap2.shape[0], ap2.shape[1], n])

        def f(ap):
            return ap.bitcast(F32)

        state = {}

        made = []
        W, IN, SA, SB, SC = (Stage(x, made) for x in (semW, semW, semA, semB, semC))

        def load(dst, src, s, after=(), cost=None):
            return W.put("sp", SY.dma_start, dst, src, sem=s, by=16, after=after, cost=cost)

        def wide(v, n=P):
            return v.rearrange("(a n) -> a n", a=1).to_broadcast([n, v.shape[0]])

        zi = W.put("pool", G.memset, ident[:], 0.0)
        zi2 = W.put("pool", G.affine_select, out=ident[:], in_=ident[:], compare_op=ALU.not_equal,
                    fill=1.0, base=0, pattern=[[-1, P]], channel_multiplier=1, after=[zi])
        id_r = W.put("pool", G.tensor_copy, ident_r[:], ident[:], after=[zi2])
        id_b = W.put("pool", G.tensor_copy, ident_b[:], ident[:], after=[zi2])
        zc = W.put("pool", G.memset, causal[:], 0.0)
        cq = W.put("pool", G.affine_select, out=causal[:], in_=causal[:], compare_op=ALU.is_ge,
                   fill=MASKED, base=0, pattern=[[-1, P]], channel_multiplier=1, after=[zc])
        c1 = W.put("pool", G.memset, ones32[:], 1.0)
        ones_done = W.put("act", A.activation, ones_r[:], causal[:], ACT.Identity, bias=1.0, scale=0.0,
                          after=[cq])
        c2 = W.put("pool", G.memset, minus_half[:], -0.5)
        for e in range(NE):
            c3 = W.put("pool", G.memset, earlier[:, e:e + 1], float(NE - e))
        z0 = W.put("pool", G.memset, WqS0[:], 0.0)
        z1 = W.put("pool", G.memset, WkS0[:], 0.0)
        z2 = W.put("pool", G.memset, WqS1[:], 0.0)
        z3 = W.put("pool", G.memset, WkS1[:], 0.0)
        zq = W.put("dve", V.memset, MtA[:], 0.0)
        zr = W.put("dve", V.memset, MtB[:].bitcast(F32), 0.0)
        zbd = W.put("dve", V.memset, bdA[:], 0.0)
        zv = W.put("dve", V.memset, Vaug[:, :, HD:HD + 1], 1.0)
        zv1 = W.put("dve", V.memset, Vaug1[:, :, HD:HD + 1], 1.0)

        rows3 = PTB[0:1, 0].rearrange("p t (j s) -> p t j s", j=NJ)
        w0 = W.put("dve", V.memset, rows3, 0.0)
        wa = W.put("dve", V.memset, rows3[:, 0, :, MROW1:MROW1 + 2], 1.0, after=[w0])
        wb = W.put("dve", V.memset, rows3[:, 1, :, 2 * HD:3 * HD], -1.0, after=[w0])
        wc = W.put("dve", V.memset, rows3[:, 2, :, HD:2 * HD], -1.0, after=[w0])
        wd = W.put("dve", V.memset, rows3[:, 2, :, MROW1:MROW1 + 2], 1.0, after=[w0])
        we = W.put("dve", V.memset, rows3[:, 3, :, MROW0:MROW0 + 2], 1.0, after=[w0])
        bias_rows = PTB[0:NT, 1, 0:2].rearrange("p n (j s) -> p n j s", j=NJ)
        zb = W.put("dve", V.memset, bias_rows, 0.0)
        wq0_raw = raw[:, 0, 0:P]
        wk0_raw = raw[:, 0, P:2 * P]
        wv0_raw = raw[:, 0, 2 * P:3 * P]
        wo0_raw = raw[:, 0, 3 * P:4 * P]
        wq1_raw = raw[:, 0, 4 * P:5 * P]
        wk1_raw = raw[:, 0, 5 * P:6 * P]
        bv_raw = raw[:, 0, 6 * P:7 * P]
        bo_raw = raw[:, 0, 7 * P:8 * P]
        sel_raw = raw[:, 1, 0:P]
        def loads_of(s, pairs, after=()):
            for dst, src in pairs:
                got = load(dst, src, s, after=after)
            return got

        biases_in = loads_of(s_weights[0], (
            (bias_rows[:, n, :, 0:HD], v.rearrange("(t j d) -> t j d", j=NJ, d=HD)) for n, v in enumerate((bq0, bk0))),
            after=[zb])
        attn0_in = loads_of(s_weights[1], (
            (wk0_raw, Wk0), (wq0_raw, Wq0), (wv0_raw, Wv0), (bv_raw, wide(bv0)), (wo0_raw, Wo0), (bo_raw, wide(bo0))))
        attn1_in = loads_of(s_weights[2], (
            (wk1_raw, wk1.rearrange("d n h -> d (n h)")), (wq1_raw, wq1.rearrange("d n h -> d (n h)")),
            (Wv1s[:], wv1.rearrange("d n h -> d (n h)")), (Wo1s[:], wo1.rearrange("n h d -> (n h) d"))))
        ffn0_in = loads_of(s_weights[3], (
            (Wrs[:], Wr), (W1s[:], W1.rearrange("e d f -> d e f")), (Ws1s[:], Ws1), (Ws2s[:], Ws2),
            (W2s[:], W2.rearrange("(a e) f d -> (e f) a d", a=NPAIR))))
        switch_in = loads_of(s_weights[4], (
            (sel_raw[0:G1, :], selv_w), (sel_raw[G1:2 * G1, :], selo_w), (rs[:], wide(rscale))))

        sc = W.put("act", A.activation, WqS0[:, :, 0:HD], wq0_raw.rearrange("p (n d) -> p n d", d=HD),
                   ACT.Copy, after=[attn0_in, z0])
        sc = W.put("act", A.activation, WkS0[:, :, 0:HD], wk0_raw.rearrange("p (n d) -> p n d", d=HD),
                   ACT.Copy, after=[z1])
        sc = W.put("act", A.activation, Wv0b[:], wv0_raw, ACT.Copy)
        sc = W.put("act", A.activation, Wo0b[:], wo0_raw, ACT.Copy)
        sc = W.put("act", A.activation, bvb[:], bv_raw, ACT.Copy)
        scaled0 = W.put("act", A.activation, bob[:], bo_raw, ACT.Copy)
        for r in range(3):
            sc = W.put("act", A.mul, WqS1[:, :, r * HD:(r + 1) * HD],
                       wq1_raw.rearrange("p (n d) -> p n d", d=HD), SCALE0, after=[z2, attn1_in])
            sc = W.put("act", A.activation, WkS1[:, :, r * HD:(r + 1) * HD],
                       wk1_raw.rearrange("p (n d) -> p n d", d=HD), ACT.Copy, after=[z3])
        scaled = sc
        for n in range(4):
            tr = mm(W, psA[:, 0, n:n + 1], rows3[:, n].rearrange("a j s -> a (j s)"), ones32[0:1, 0:1],
                    True, True, after=[wa, wb, wc, wd, we, c1])
        tb = mm(W, psA[:, 0, 8:8 + NT], bias_rows[:, 0].rearrange("t j s -> t (j s)"), ident[0:NT, 0:NT],
                True, True, after=[biases_in, zb, zi2])
        tb = mm(W, psA[:, 0, 16:16 + NT], bias_rows[:, 1].rearrange("t j s -> t (j s)"), ident[0:NT, 0:NT],
                True, True)
        d1 = W.put("dve", V.tensor_copy, one_row[:], psA[:, 0, 0:1], after=[tb])
        d1 = W.put("dve", V.tensor_copy, less_q[:], psA[:, 0, 1:2])
        d1 = W.put("dve", V.tensor_copy, less_k[:], psA[:, 0, 2:3])
        d0 = W.put("dve", V.tensor_copy, max_rows[:], psA[:, 0, 3:4])
        d1 = W.put("dve", V.tensor_copy, bqS[:], psA[:, 0, 8:8 + NT])
        columns_done = W.put("dve", V.tensor_scalar, bkS[:], psA[:, 0, 16:16 + NT], max_rows[:], None, ALU.add,
                   after=[d0])
        ts = W.put("pe", T.transpose, psB[:, 0, 0:P], sel_raw, ident[:], after=[switch_in, zi2])
        small_done = W.put("dve", V.tensor_copy, selT[:], psB[:, 0, 0:P], after=[ts])

        qload = load(raw[:, 0, :].rearrange("p (h d) -> p h d", h=H1),
                     q_w.rearrange("(h p) d -> p h d", p=P), s_raw[0], after=[scaled])
        kload = load(raw[:, 1, :].rearrange("p (h d) -> p h d", h=H1),
                     k_w.rearrange("(h p) d -> p h d", p=P), s_raw[1], after=[ts])
        for h in range(H1):
            mh = mm(W, psC[:, 0, h * P:(h + 1) * P], raw[:, 0, h * P:(h + 1) * P],
                    raw[:, 1, h * P:(h + 1) * P], True, True, after=[qload, kload])
        Mdone = W.put("act", A.activation, M[:].rearrange("p h d -> p (h d)"), psC[:, 0, :], ACT.Copy,
                      after=[mh])
        last_read = [Mdone, Mdone]
        cut_done = {}
        n = 0
        for name, src, hi_sb, lo_sb in (("v", v_w, Vh, Vl), ("o", o_w, Oh, Ol)):
            for h in range(H1):
                k = n % 2
                got = load(raw[:, k, :].rearrange("p (e n) -> p e n", e=NE),
                           src[h * NE:(h + 1) * NE].rearrange("e p n -> p e n"), s_raw[k],
                           after=[last_read[k]], cost=1700.0)
                for e in (h * NE, h * NE + NE // 2):
                    hsl = hi_sb[:, e:e + NE // 2, :].rearrange("p e n -> p (e n)")
                    lsl = lo_sb[:, e:e + NE // 2, :].rearrange("p e n -> p (e n)")
                    part = raw[:, k, (e - h * NE) * P:(e - h * NE + NE // 2) * P]
                    hi = W.put("act", A.activation, hsl, part, ACT.Copy, after=[got])
                    lo = W.put("dve", V.tensor_tensor, lsl, part, f(hsl), ALU.subtract, after=[hi, got])
                last_read[k] = lo
                cut_done[name, h] = lo
                n += 1
        state["bdB_zero"] = W.put("dve", V.memset, bdB[:].bitcast(F32), 0.0, after=last_read)

        def layernorm(st, x, stats, mv, rstd, dst, after):
            a = st.put("dve", V.bn_stats, stats[:], x, after=after)
            a = st.put("dve", V.bn_aggr, mv[:], stats[:], after=[a])
            p = st.put("dve", V.tensor_scalar, rstd[:], mv[:, 1:2], EPS, None, ALU.add, after=[a])
            p = st.put("pool", G.tensor_tensor, rstd[:], rstd[:], minus_half[:], ALU.pow, after=[p, c2])
            return st.put("dve", V.tensor_scalar, dst[:], x, mv[:, 0:1], rstd[:], ALU.subtract, ALU.mult,
                          after=[p])

        def since(*keys):
            return [state[k] for k in keys if k in state]

        def loads(b):
            k = b % 2
            for key, dst, src in (("x1", x_sb[:, k], x_in[b]), ("ctx", ctx_sb[:, k], ctx_in[b]),
                                  ("mask", mrow_i[:, k], wide(mask_in[b])),
                                  ("mask", mcol_i[:, k], mask_in[b].rearrange("(s a) -> s a", a=1))):
                state["in", b] = IN.put("sp", SY.dma_start, dst, src, sem=s_in[k], by=16,
                                        after=since((key, b - 2)))

        def load_bias(b):
            state["inbias", b] = IN.put("sp", SY.dma_start, bias_sb[:, b % 2], bias_in[b, 0],
                                        sem=s_bias[b % 2], by=16, after=since(("bias", b - 2)))

        def slot_blocks(slots, bd):
            for j in range(NJ):
                rows_j = slice(SLOT * j, SLOT * (j + 1))
                yield bd[rows_j, :, j, :], slots[rows_j]

        def attend(st, ps, free, Qslot, Kslot, Qwithmax, bd, kd, Mt, nm, PT, Vp, U, at, rden,
                   mask_q, mask_k, mrow, scale, ident_mm, ready, vready, key_bias=None):
            def scores(t, bank, tiles, pairs, spread_done, after):
                o = ps[:, bank, :].rearrange("p (j s) -> p j s", j=NJ)
                for n, (l, r) in enumerate(pairs):
                    mm(st, o, l, r, n == 0, False, after=after)
                return mm(st, o, tiles[:, t, :], bd[:, t], not pairs, True,
                          after=[spread_done] if pairs else [spread_done, *after])

            for t in range(NT):
                bank = t % 2
                s = scores(t, bank, Qslot, mask_q, kd, [*ready, *free[bank]])
                m = st.put("dve", V.tensor_reduce, nm[:, t, :], ps[:, bank, :].rearrange("p (j s) -> p j s", j=NJ),
                           AX_X, ALU.max, negate=True, after=[s])
                free[bank] = [m]
            hv = Mt[:, :, :, mrow]
            hi = st.put("dve", V.tensor_copy, hv, nm[:], after=[m])
            lo = st.put("dve", V.tensor_tensor, Mt[:, :, :, mrow + 1], nm[:],
                        f(hv) if Mt.dtype == F32R else hv, ALU.subtract, after=[hi])
            for t in range(NT):
                tp = mm(st, ps[:, 0, t * P:(t + 1) * P], Mt[:, t].rearrange("p j s -> p (j s)"), ident_mm,
                        True, True, after=[lo, *free[0]])
            q = f(Qslot[:]) if Qslot.dtype == F32R else Qslot[:]
            q2 = st.put("dve", V.tensor_tensor, Qwithmax[:], ps[:, 0, :].rearrange("p (t s) -> p t s", t=NT),
                        q, ALU.add, after=[tp])
            free[0] = [q2]
            for to, frm in slot_blocks(Qwithmax, bd):
                qd = st.put("dve", V.tensor_copy, to, frm, after=[q2, s],
                            cost=COST["dve"][0] + NT * P * (0.26 if bd.dtype == BF16 else 0.52))
            used = [[], []]
            for t in range(NT):
                s = scores(t, 1, Kslot, mask_k, qd, [*free[1]])
                e = st.put("act", A.activation, PT[:, t % 2].rearrange("p t s -> p (t s)"), ps[:, 1, :],
                           ACT.Exp, scale=scale, after=[s, *used[t % 2]],
                           **({} if key_bias is None else {"bias": key_bias}))
                free[1] = [e]
                if key_bias is not None:
                    e = st.put("pool", G.affine_select, out=PT[:, t % 2], in_=PT[:, t % 2],
                               compare_op=ALU.is_ge, fill=0.0, base=0, pattern=[[0, NJ], [1, P]],
                               channel_multiplier=-1, after=[e])
                for j in range(NJ):
                    pv = mm(st, ps[SLOT * j:SLOT * j + HD + 1, 0, t * P:(t + 1) * P], Vp[:, NJ * t + j, :],
                            PT[:, t % 2, j, :], True, True, after=[e, vready, *free[0]])
                used[t % 2] = [pv]
            u = st.put("act", A.activation, U, ps[:, 0, :], ACT.Copy, after=[pv])
            free[0] = [u]
            for t in range(NT):
                tp = st.put("pe", T.transpose, ps[:, 1, t * P:(t + 1) * P], U[:, t * P:(t + 1) * P], ident[:],
                            after=[u, *free[1]])
            o = ps[:, 1, :].rearrange("p (n w) -> p n w", n=NH)
            r = st.put("dve", V.reciprocal, rden[:], o[:, :, HD], after=[tp])
            a = st.put("dve", V.tensor_tensor, at[:], o[:, :, 0:HD], along(rden[:], HD), ALU.mult, after=[r])
            free[1] = [a]
            return a, s

        freeA = {0: [columns_done], 1: [columns_done]}
        freeB = {0: [small_done], 1: []}
        freeC = [[[Mdone], [Mdone]], [[Mdone], [Mdone]]]
        s_bdA, s_bdB = sem("bdA"), sem("bdB")

        def stage_a(b):
            st = SA
            k = b % 2
            x = x_sb[:, k]
            loaded = state["in", b]
            mk = st.put("pool", G.tensor_scalar, keyrow[:], mrow_i[:, k], 0, MASKED, ALU.is_le, ALU.mult,
                        after=[loaded, cq, *since(("maskused", b - 1))])
            mk1 = st.put("pool", G.tensor_scalar, keycol[:], mcol_i[:, k], 0, MASKED, ALU.is_le, ALU.mult)
            mk2 = st.put("pool", G.tensor_tensor, maskq[:], keyrow[:], causal[:], ALU.add, after=[mk])
            state["mask", b] = mk1
            n = layernorm(st, x, stA, mvA, rsA, xnbA, [loaded])
            tc = st.put("pe", T.transpose, psA[:, 1, 0:P], ctx_sb[:, k], ident[:], after=[loaded, zi2, *freeA[1]])
            state["ctx", b] = tc
            cb = st.put("act", A.activation, ctxTb[:], psA[:, 1, 0:P], ACT.Copy, after=[tc])
            cc = st.put("act", A.activation, ctxT[:, k], psA[:, 1, 0:P], ACT.Copy,
                        after=since(("ctxTused", b - 2)))
            state["ctxT", b] = cc
            wq = WqS0[:].rearrange("p n s -> p (n s)")
            wk = WkS0[:].rearrange("p n s -> p (n s)")
            for t in range(NT):
                kk = mm(st, psA[:, 1, t * P:(t + 1) * P], wk[:, t * P:(t + 1) * P], ctxTb[:], True, True,
                        after=[cc, scaled0])
            kb = st.put("act", A.activation, Kb.rearrange("p t s -> p (t s)"), psA[:, 1, :], ACT.Copy,
                        after=[kk])
            ks = st.put("pool", G.tensor_tensor, Ks[:], Kb, along(bkS[:], P), ALU.add, after=[kb, columns_done])
            for to, frm in slot_blocks(Ks, bdA):
                kd = st.put("sp", SY.dma_start, to, frm, sem=s_bdA, by=16,
                            after=[ks, zbd, *since(("bdA", b - 1))])
            v = mm(st, psA[:, 1, 0:P], ctxTb[:], Wv0b[:], True, True, after=[kb])
            vb = st.put("act", A.activation, Vb[:], psA[:, 1, 0:P], ACT.Copy, after=[v])
            vb2 = st.put("pool", G.tensor_tensor, Vb2[:], Vb[:], bvb[:], ALU.add, after=[vb, scaled0])
            va = st.put("act", A.activation, Vaug[:, :, 0:HD], Vb2[:].rearrange("p (n d) -> p n d", d=HD), ACT.Copy,
                        after=[vb2, zv])
            psb = psA[:, 0, 0:64].bitcast(BF16)
            tp = st.put("pe", T.transpose, psb, xnbA[:], ident_b[:], after=[n, id_b, *freeA[0]])
            c = st.put("act", A.activation, xTbA[:], psb, ACT.Copy, after=[tp])
            for t in range(NT):
                q = mm(st, psA[:, 0, t * P:(t + 1) * P], wq[:, t * P:(t + 1) * P], xTbA[:], True, True, after=[c])
            qb = st.put("act", A.activation, Qb.rearrange("p t s -> p (t s)"), psA[:, 0, :], ACT.Copy,
                        after=[q])
            qs = st.put("pool", G.tensor_tensor, Qs[:], Qb, along(bqS[:], P), ALU.add, after=[qb])
            free = {0: [qb], 1: [vb]}
            a, bd_read = attend(st, psA, free, Qs, Ks, Q2, bdA, kd, MtA, nmA, PTA, Vaug, UA, atb, rdA,
                       [(ident_b[:], over_heads(maskq[:], NT))], [], MROW0, SCALE0, ident_b[:], [qs, mk2, zq], va,
                       keycol[:])
            state["bdA", b] = bd_read
            tp = st.put("pe", T.transpose, psA[:, 1, 0:64].bitcast(BF16), atb[:].rearrange("p n d -> p (n d)"),
                        ident_b[:], after=[a, *free[1]])
            state["maskused", b] = tp
            c = st.put("act", A.activation, atTb[:], psA[:, 1, 0:64].bitcast(BF16), ACT.Copy, after=[tp])
            o = mm(st, psA[:, 0, 0:P], atTb[:], Wo0b[:], True, True, after=[c, *free[0]])
            ob = st.put("act", A.activation, obA[:], psA[:, 0, 0:P], ACT.Copy, after=[o])
            o2 = st.put("dve", V.tensor_tensor, ob2[:], obA[:], bob[:], ALU.add, after=[ob])
            xx = st.put("dve", V.tensor_tensor, x1[:], x, ob2[:], ALU.add, after=[o2])
            state["x1", b] = xx
            n = layernorm(st, x1[:], stA, mvA, rsA, xnA, [xx])
            tp = st.put("pe", T.transpose, psA[:, 1, 0:P], xnA[:], ident[:], after=[n])
            xt = st.put("act", A.activation, xTA[:], psA[:, 1, 0:P], ACT.Copy, after=[tp])
            rl = mm(st, psA[:, 0, 0:E0], xTA[:], Wrs[:], True, True, after=[xt, ffn0_in])
            l = st.put("dve", V.tensor_copy, lg[:], psA[:, 0, 0:E0], after=[rl])
            t8 = st.put("dve", V.max, top8[:], lg[:], after=[l])
            gp_ = st.put("dve", V.tensor_tensor, gap[:], top8[:, 1:2], top8[:, 0:1], ALU.subtract, after=[t8])
            hid = mm(st, psA[:, 1, :], xTA[:], W1s[:].rearrange("p e f -> p (e f)"), True, True)
            sh = mm(st, psA[0:F0, 0, 0:P], Ws1s[:], xTA[:], True, True, after=[l])
            eg = st.put("act", A.activation, egap[:], gap[:], ACT.Exp, after=[gp_])
            r_ = st.put("act", A.activation, hs[:], psA[0:F0, 0, 0:P], ACT.Relu, after=[sh])
            r2_ = st.put("act", A.activation, hs2[:], hs[:], ACT.Square, after=[r_])
            su = st.put("dve", V.tensor_scalar, sure[:], egap[:], 1.0, 1.0, ALU.add, ALU.is_equal, after=[eg])
            pr = st.put("dve", V.tensor_scalar, prob[:], lg[:], top8[:, 0:1], sure[:], ALU.is_equal, ALU.mult,
                        after=[su])
            hgs = st.put("dve", V.scalar_tensor_tensor, hg, psA[:, 1, :].rearrange("p (e f) -> p e f", e=E0),
                         0.0, along(prob[:], F0), ALU.max, ALU.mult, after=[pr, hid])
            hgf = hg.rearrange("p e f -> p (e f)")
            for a_ in range(NPAIR):
                tp = st.put("pe", T.transpose, psA[:, 1, a_ * P:(a_ + 1) * P], hgf[:, a_ * P:(a_ + 1) * P],
                            ident[:], after=[hgs])
            hq = st.put("act", A.activation, hT.rearrange("p a s -> p (a s)"), psA[:, 1, :], ACT.Square,
                        after=[tp])
            mm(st, psA[:, 0, 0:P], hs2[:], Ws2s[:], True, False, after=[r2_])
            for a_ in range(NPAIR):
                y = mm(st, psA[:, 0, 0:P], hT[:, a_, :], W2s[:, a_, :], False, a_ == NPAIR - 1, after=[hq])
            xo = st.put("dve", V.tensor_tensor, x2[:, k], psA[:, 0, 0:P], x1[:], ALU.add,
                        after=[y, *since(("x2used", b - 2))])
            state["x2", b] = xo
            freeA[0], freeA[1] = [xo], [hq]

        def stage_b(b):
            st = SB
            k = b % 2
            x = x2[:, k]
            loaded = state["inbias", b]
            b0 = st.put("act", A.activation, bh[:], bias_sb[:, k], ACT.Copy, after=[loaded, *since(("biasused", b - 1))])
            b1 = st.put("pool", G.tensor_tensor, bl[:], bias_sb[:, k], f(bh[:]), ALU.subtract, after=[b0])
            state["bias", b] = b1
            wq = WqS1[:].rearrange("p n s -> p (n s)")
            wk = WkS1[:].rearrange("p n s -> p (n s)")
            Qh1f = Qh1[:].rearrange("p t s -> p (t s)")
            for t in range(NT):
                kk = mm(st, psB[:, 1, t * P:(t + 1) * P], wk[:, t * P:(t + 1) * P], ctxT[:, k], True, True,
                        after=[scaled, state["ctxT", b], *freeB[1]])
            kh = st.put("act", A.activation, Qh1f.bitcast(F32R), psB[:, 1, :], ACT.Identity, bias=one_row[:],
                        after=[kk, columns_done])
            k2 = st.put("dve", V.scalar_tensor_tensor, Ks1[:].rearrange("p t s -> p (t s)"), Qh1f, less_k[:],
                        psB[:, 1, :], ALU.mult, ALU.add, after=[kh])
            for to, frm in slot_blocks(Ks1, bdB):
                kd = st.put("sp", SY.dma_start, f(to), f(frm), sem=s_bdB, by=16,
                            after=[k2, state["bdB_zero"], *since(("bdB", b - 1))])
            v = mm(st, psB[:, 1, 0:P], ctxT[:, k], Wv1s[:], True, True, after=[k2, attn1_in])
            state["ctxTused", b] = v
            va = st.put("act", A.activation, Vaug1[:, :, 0:HD],
                        psB[:, 1, 0:P].rearrange("p (n d) -> p n d", d=HD), ACT.Copy, after=[v, zv1])
            n = layernorm(st, x, stB, mvB, rsB, xnB, [state["x2", b]])
            tp = st.put("pe", T.transpose, psB[:, 0, 0:P], xnB[:], ident[:], after=[n, zi2, *freeB[0]])
            c = st.put("act", A.activation, xTB[:], psB[:, 0, 0:P], ACT.Copy, after=[tp])
            for t in range(NT):
                q = mm(st, psB[:, 0, t * P:(t + 1) * P], wq[:, t * P:(t + 1) * P], xTB[:], True, True, after=[c])
            qh = st.put("act", A.activation, Qh1f.bitcast(F32R), psB[:, 0, :], ACT.Copy, after=[q, k2])
            q2 = st.put("dve", V.scalar_tensor_tensor, Qs1[:].rearrange("p t s -> p (t s)"), Qh1f, less_q[:],
                        psB[:, 0, :], ALU.mult, ALU.add, after=[qh])
            free = {0: [q2], 1: [va]}
            a, bd_read = attend(st, psB, free, Qs1, Ks1, Q21, bdB, kd, MtB, nmB, PTB, Vaug1, Qh1f, atB, rdB,
                       [(ident_r[:], over_heads(bh[:], NT)), (ident_r[:], over_heads(bl[:], NT))],
                       [(bh[:], over_heads(ident_r[:], NT)), (bl[:], over_heads(ident_r[:], NT))],
                       MROW1, 1.0, ident_r[:], [q2, b1, id_r, zr], va)
            state["bdB", b] = bd_read
            tp = st.put("pe", T.transpose, psB[:, 1, 0:P], atB[:].rearrange("p n d -> p (n d)"), ident[:],
                        after=[a, *free[1]])
            state["biasused", b] = tp
            c = st.put("act", A.activation, atTB[:], psB[:, 1, 0:P], ACT.Copy, after=[tp])
            o = mm(st, psB[:, 0, 0:P], atTB[:], Wo1s[:], True, True, after=[c, *free[0]])
            xo = st.put("dve", V.tensor_tensor, x3[:, k], psB[:, 0, 0:P], x, ALU.add,
                        after=[o, *since(("x3used", b - 2))])
            state["x2used", b] = xo
            state["x3", b] = xo
            freeB[0], freeB[1] = [xo], [c]

        turn = [0]

        parity = [0]

        def pair():
            p = turn[0] % 2
            turn[0] += 1
            return psC[:, p], p

        def experts(lhs, w_hi, w_lo, h, g_of, gates_ready, after):
            st = SC
            i = parity[0] % RING
            parity[0] += 1
            ps, p = pair()
            for half in (1, 0):
                o = ps[:, 512 * half:512 * half + 512]
                e0 = h * NE + half * (NE // 2)
                wh = w_hi[:, e0:e0 + NE // 2].rearrange("p e n -> p (e n)")
                wl = w_lo[:, e0:e0 + NE // 2].rearrange("p e n -> p (e n)")
                mm(st, o, lhs[0], wh, True, False, after=[*after, *freeC[p][half]])
                mm(st, o, lhs[1], wh, False, False)
                z = mm(st, o, lhs[2], wl, False, True)
                if half:
                    z1_ = z
            te = []
            for e in range(NE // 2):
                te.append(st.put("act", A.activation, TE[:, i, e], ps[:, 512 + e * P:512 + (e + 1) * P],
                                 ACT.Copy, scale=g_of(h, e + NE // 2),
                                 after=[z1_, gates_ready, *since(("fe", i))]))
            for e in range(NE // 2):
                de = st.put("dve", V.scalar_tensor_tensor, DE[:, i, e], ps[:, e * P:(e + 1) * P],
                            g_of(h, e), TE[:, i, e], ALU.mult, ALU.add,
                            after=[z, te[e], gates_ready, *since(("fe", i))])
            freeC[p][:] = [de], [te[-1]]
            state["de", i] = de
            return i, de

        def head(b):
            st = SC
            k = b % 2
            x = x3[:, k]
            n = layernorm(st, x, stC, mvC, rsC, xnC, [state["x3", b]])
            yield
            ps, p = pair()
            tp = st.put("pe", T.transpose, ps[:, 0:P], xnC[:], ident[:], after=[n, zi2, *freeC[p][0]])
            h_ = st.put("act", A.activation, xTh[:], ps[:, 0:P], ACT.Copy, after=[tp])
            c = st.put("act", A.activation, xTC[:], ps[:, 0:P], ACT.Copy)
            xb_ = st.put("act", A.activation, xTb[:], ps[:, 0:P], ACT.Copy)
            l_ = st.put("dve", V.tensor_tensor, xTl[:], ps[:, 0:P], f(xTh[:]), ALU.subtract, after=[h_, xb_])
            gl = mm(st, ps[:, 512:512 + 2 * G1], xTC[:], selT[:], True, True,
                    after=[c, small_done, *freeC[p][1]])
            gpf = gp[:].rearrange("p g e -> p (g e)")
            e_ = st.put("act", A.activation, gpf, ps[:, 512:512 + 2 * G1], ACT.Exp, scale=-1.0, after=[gl])
            freeC[p][:] = [l_], [e_]
            g = st.put("dve", V.tensor_scalar, gpf, gpf, -1.0, -1.0, ALU.mult, ALU.add, after=[e_])
            yield
            ps, p = pair()
            for h in range(H1):
                y = mm(st, ps[:, h * P:(h + 1) * P], M[:, h], xTC[:], True, True, after=[c, Mdone, *freeC[p][h // 4]])
                if h % 4 == 3:
                    i = h // 4
                    yhf = yh[:, 4 * i:4 * i + 4].rearrange("p h s -> p (h s)")
                    ylf = yl[:, 4 * i:4 * i + 4].rearrange("p h s -> p (h s)")
                    yy = st.put("act", A.activation, yhf, ps[:, 512 * i:512 * i + 512], ACT.Copy, after=[y])
                    yx = st.put("dve", V.tensor_tensor, ylf, ps[:, 512 * i:512 * i + 512], f(yhf), ALU.subtract,
                                after=[yy])
                    freeC[p][i] = [yx]
            g = st.put("dve", V.tensor_reduce, m1, gp[:], AX_X, ALU.max, after=[g])

            def first_best(src, best, dst, after):
                a = st.put("dve", V.tensor_tensor, gt[:], src[:], along(best, NE), ALU.is_equal, after=after)
                a = st.put("dve", V.tensor_tensor, gt[:], gt[:], over_heads(earlier[:], 2 * H1), ALU.mult,
                           after=[a, c3])
                a = st.put("dve", V.tensor_reduce, r1[:], gt[:], AX_X, ALU.max, after=[a])
                return st.put("dve", V.tensor_tensor, dst[:], gt[:], along(r1[:], NE), ALU.is_equal, after=[a])

            g = first_best(gp, m1, first, [g])
            yield
            ps, p = pair()
            for h in range(H1):
                s = mm(st, ps[:, h * P:(h + 1) * P], yh[:, h], xTh[:], True, True, after=[yy, *freeC[p][h // 4]])
            g = st.put("dve", V.scalar_tensor_tensor, gp2[:].rearrange("p g e -> p (g e)"),
                       first[:].rearrange("p g e -> p (g e)"), TAKEN, gpf, ALU.mult, ALU.add, after=[g])
            g = st.put("dve", V.tensor_reduce, m2, gp2[:], AX_X, ALU.max, after=[g])
            g = first_best(gp2, m2, second, [g])
            dg = []
            for i in range(H1 // 4):
                four = slice(4 * i, 4 * i + 4)
                nm = st.put("dve", V.tensor_reduce, nmC[:, four],
                            ps[:, 512 * i:512 * i + 512].rearrange("p (h s) -> p h s", h=4), AX_X,
                            ALU.max, negate=True, after=[s])
                dg.append(st.put("pool", G.tensor_tensor, lessmax[:, four], over_heads(ident[:], 4),
                                 along(nmC[:, four], P), ALU.mult, after=[nm, *since(("lessmax", b - 1))]))
                freeC[p][i] = [nm]
            both = best2[:].rearrange("p n g -> p (n g)")
            q = st.put("dve", V.reciprocal, both, both, after=[g])
            q = st.put("dve", V.tensor_tensor, gsum[:], m1, m2, ALU.add, after=[q])
            q = st.put("dve", V.tensor_scalar, gsum[:], gsum[:], -1e-9, None, ALU.min, after=[q])
            q = st.put("dve", V.reciprocal, gsum[:], gsum[:], after=[q])
            q = st.put("dve", V.tensor_scalar, gsum[:], gsum[:], rs[:], None, ALU.mult, after=[q, switch_in])
            q1 = st.put("dve", V.tensor_tensor, m1, m1, gsum[:], ALU.mult, after=[q])
            q2 = st.put("dve", V.tensor_tensor, m2, m2, gsum[:], ALU.mult, after=[q])
            q1 = st.put("pool", G.tensor_tensor, first[:], first[:], along(m1, NE), ALU.mult, after=[q2])
            q2 = st.put("pool", G.tensor_tensor, second[:], second[:], along(m2, NE), ALU.mult)
            gt_ = st.put("pool", G.tensor_tensor, gate[:], first[:], second[:], ALU.add, after=[q1, q2])
            yield
            ps, p = pair()
            for i in range(H1 // 4):
                o = ps[:, 512 * i:512 * i + 512]
                yhf = yh[:, 4 * i:4 * i + 4].rearrange("p h s -> p (h s)")
                ylf = yl[:, 4 * i:4 * i + 4].rearrange("p h s -> p (h s)")
                mm(st, o, xTh[:], yhf, True, False, after=[*freeC[p][i]])
                mm(st, o, xTh[:], ylf, False, False, after=[yx])
                mm(st, o, xTl[:], yhf, False, False)
                s = mm(st, o, ones_r[:], lessmax[:, 4 * i:4 * i + 4].rearrange("p h s -> p (h s)"), False, True,
                       after=[dg[i], ones_done])
                ex = st.put("act", A.activation, PTC[:, 4 * i:4 * i + 4].rearrange("p h s -> p (h s)"), o,
                            ACT.Exp, scale=SCALE1, after=[s])
                freeC[p][i] = [ex]
            state["lessmax", b] = ex

            state["C", b] = ex, xb_, gt_

        def values(b):
            st = SC
            ex, xb_, gt_ = state["C", b]
            summed = []
            for h in range(H1):
                i, de = experts((xTh[:], xTl[:], xTb[:]), Vh, Vl, h, lambda h, e: gate[:, h, e:e + 1], gt_,
                                [cut_done["v", h], xb_])
                fe = st.put("pool", G.tensor_tensor, DE[:, i, 0:2], DE[:, i, 0:2], DE[:, i, 2:4], ALU.add, after=[de])
                vv = st.put("pool", G.tensor_tensor, v_sb[:, h], DE[:, i, 0], DE[:, i, 1], ALU.add, after=[fe])
                state["fe", i] = vv
                summed.append(vv)
                yield
                if h == 4:
                    ps, p = pair()
                    for hh in range(H1):
                        j, t = hh % NJ, hh // NJ
                        dn = mm(st, ps[SLOT * j:SLOT * (j + 1), t * P:(t + 1) * P], ones32[:], PTC[:, hh], True, True,
                                after=[ex, c1, *freeC[p][0]])
                    dc = st.put("act", A.activation, den[:].rearrange("p t s -> p (t s)"), ps[:, 0:H1 // NJ * P],
                                ACT.Copy, after=[dn])
                    for t in range(H1 // NJ):
                        dn = st.put("pe", T.transpose, ps[:, 512 + t * P:512 + (t + 1) * P], den[:, t], ident[:],
                                    after=[dc, *freeC[p][1]])
                    rd = st.put("dve", V.reciprocal, rdC[:],
                                ps[:, 512:512 + H1 * SLOT].rearrange("p (h s) -> p h s", s=SLOT)[:, :, 0],
                                after=[dn])
                    go = st.put("dve", V.tensor_tensor, gateO[:], gate[:, H1:2 * H1], along(rdC[:], NE), ALU.mult,
                                after=[rd, gt_])
                    freeC[p][:] = [dc], [rd]
            cut = []
            ps, p = pair()
            for h in range(H1):
                o = mm(st, ps[:, h * P:(h + 1) * P], v_sb[:, h], PTC[:, h], True, True, after=[summed[h], *freeC[p][h // 4]])
                if h % 4 == 3:
                    i = h // 4
                    chf = ch[:, 4 * i:4 * i + 4].rearrange("p h s -> p (h s)")
                    clf = cl[:, 4 * i:4 * i + 4].rearrange("p h s -> p (h s)")
                    cbf = cb_[:, 4 * i:4 * i + 4].rearrange("p h s -> p (h s)")
                    cx = st.put("act", A.activation, chf, ps[:, 512 * i:512 * i + 512], ACT.Copy, after=[o])
                    cz = st.put("act", A.activation, cbf, f(chf), ACT.Copy, after=[cx])
                    cy = st.put("dve", V.tensor_tensor, clf, ps[:, 512 * i:512 * i + 512], f(chf), ALU.subtract,
                                after=[cx])
                    freeC[p][i] = [cy]
                    cut.append([cy, cz])
            state["context", b] = go, cut

        def output(b):
            st = SC
            k = b % 2
            x = x3[:, k]
            go, cut = state["context", b]
            for h in range(H1):
                i, de = experts((ch[:, h], cl[:, h], cb_[:, h]), Oh, Ol, h, lambda h, e: gateO[:, h, e:e + 1], go,
                                [*cut[h // 4], cut_done["o", h]])
                if h:
                    before = accO[:] if h > 1 else DE[:, first_i]
                    fe = st.put("pool", G.tensor_tensor, accO[:], before, DE[:, i], ALU.add,
                                after=[de, *([fe] if h > 1 else since("accOread"))])
                    state["fe", i] = fe
                    if h == 1:
                        state["fe", first_i] = fe
                else:
                    first_i = i
                yield
            fe = st.put("pool", G.tensor_tensor, accO[:, 0:2], accO[:, 0:2], accO[:, 2:4], ALU.add, after=[fe])
            fe = st.put("pool", G.tensor_tensor, accO[:, 0], accO[:, 0], accO[:, 1], ALU.add, after=[fe])
            rr = st.put("pool", G.tensor_tensor, res[:], accO[:, 0], x, ALU.add,
                        after=[fe, *since(("stored", b - 1))])
            state["x3used", b] = state["accOread"] = rr
            state["stored", b] = st.put("sp", SY.dma_start, out[b], res[:], sem=s_out[k], by=16, after=[rr])

        def run(parts, count=None):
            n = 0
            while n != count and next(parts, parts) is not parts:
                n += 1

        def stage_c(b):
            if b == 0:
                nxt = head(0)
                run(nxt)
            body = values(b)
            nxt = head(b + 1) if b + 1 < B else iter(())
            run(body, 6)
            run(nxt, 1)
            run(body)
            tail = output(b)
            for some in (2, 1, 3):
                run(tail, some)
                run(nxt, 1)
            run(tail)
            run(nxt)

        loads(0)
        for i in range(B + 2):
            if i + 1 < B:
                loads(i + 1)
            if i < B:
                load_bias(i)
                stage_a(i)
            if 0 <= i - 1 < B:
                stage_b(i - 1)
            if 0 <= i - 2 < B:
                stage_c(i - 2)
        merge([IN, SC, SA, SB, W], made, engines)
        end = [state["stored", b] for b in range(max(0, B - 2), B)]

        totals = {}
        for e in engines.values():
            e.count(totals)

        block = ctx.enter_context(nc.Block())

        @block.tensor
        def _(eng):
            engines["pe"].emit()

        @block.scalar
        def _(eng):
            engines["act"].emit()

        @block.vector
        def _(eng):
            engines["dve"].emit()

        @block.gpsimd
        def _(eng):
            engines["pool"].emit()

        @block.sync
        def _(eng):
            engines["sp"].emit()
            for s in end:
                eng.wait_ge(s.sem, s.count)


_INS = ["x", "ctx_1024", "mask_BxS2_if1", "mask_Bx1xSxS2_ff0", "L0_xattn_Wq", "L0_xattn_bq", "L0_xattn_Wk",
        "L0_xattn_bk", "L0_xattn_Wv", "L0_xattn_bv", "L0_xattn_Wo", "L0_xattn_bo", "L0_ffn_Ws1", "L0_ffn_Ws2",
        "L0_ffn_W1", "L0_ffn_W2", "L0_ffn_Wr", "L1_xattn_wq", "L1_xattn_wk", "L1_xattn_wv", "L1_xattn_wo",
        "L1_ffn_q_w", "L1_ffn_k_w", "L1_ffn_v_w", "L1_ffn_o_w", "L1_ffn_sel_v_w", "L1_ffn_sel_o_w",
        "L1_ffn_route_scale"]


def kernel(**inputs):
    import numpy as np
    import concourse.bacc as bacc
    from concourse.bass_utils import run_bass_kernel_spmd

    nc = bacc.Bacc("TRN2", target_bir_lowering=False, num_devices=1)
    arrays, args = {}, []
    for name in _INS:
        a = np.ascontiguousarray(inputs[name])
        arrays[f"in_{name}"] = a
        args.append(nc.dram_tensor(f"in_{name}", a.shape, mybir.dt.from_np(a.dtype), kind="ExternalInput").ap())
    shape = inputs["x"].shape
    args.append(nc.dram_tensor("out_0", shape, F32, kind="ExternalOutput").ap())
    program(nc, *args)
    r = run_bass_kernel_spmd(nc, [arrays], core_ids=[0])
    return r.results[0]["out_0"]
```
